# Optimizing a Trainium2 kernel written in Bass

```python
import numpy as np
import jax
import jax.numpy as jnp

def _softmax(x, axis=-1):
    return jax.nn.softmax(x, axis=axis)

def _gelu(x):
    return jax.nn.gelu(x, approximate=True)

def _silu(x):
    return jax.nn.silu(x)

def _sigmoid(x):
    return jax.nn.sigmoid(x)

def _layernorm(x, axis=-1, eps=1e-05):
    m = jnp.mean(x, axis=axis, keepdims=True)
    v = jnp.var(x, axis=axis, keepdims=True)
    return (x - m) / jnp.sqrt(v + eps)

def _scatter_add(tgt, idx, src, axis=0):
    return tgt.at[idx].add(src)

def _segment_sum(src, seg, n):
    return jax.ops.segment_sum(src, seg, n)
kernel_name = 'mk_flamingo_gated_d1_seqx_r4_a04bdc'

def setup_inputs(seed: int=0):
    np.random.seed(seed)
    _w = jnp.asarray

    def _rec_inputs():
        import jax
        import jax.numpy as jnp
        _rk = jax.random.key(seed)
        x = -0.0002928 + 1 * jax.random.normal(jax.random.fold_in(_rk, 1), (16, 512, 256), jnp.float32)
        _lenS = 512 - jax.random.randint(jax.random.fold_in(_rk, 7), (16,), 0, max(1, 512 // 4) + 1, jnp.int32)
        _lenS2 = 1601 - jax.random.randint(jax.random.fold_in(_rk, 8), (16,), 0, max(1, 1601 // 4) + 1, jnp.int32)
        _ctx_1024P = jax.random.normal(jax.random.fold_in(_rk, 11), (16, 16, 256), jnp.float32)
        _ctx_1024c = jax.random.dirichlet(jax.random.fold_in(_rk, 511), 0.3 * jnp.ones((16,), jnp.float32), (16, 1601))
        _ctx_1024t = jnp.einsum('bsk,bkd->bsd', _ctx_1024c, _ctx_1024P)
        _ctx_1024t = _ctx_1024t * jax.lax.rsqrt(jnp.mean(jnp.square(_ctx_1024t)) + 1e-12) * 0.953939
        ctx_1024 = -0.000292821 + 1.00034 * (_ctx_1024t + 0.3 * jax.random.normal(jax.random.fold_in(_rk, 611), (16, 1601, 256), jnp.float32))
        _g = jax.random.normal(jax.random.fold_in(_rk, 9001), (2, 1), jnp.float32)
        _g = jnp.sign(_g) * jnp.maximum(jnp.abs(_g), 1.0) + (_g == 0) * 1.0
        g_xattn = _g[0]
        g_ffn = _g[1]
        return (x, ctx_1024, g_xattn, g_ffn)
    x, ctx_1024, g_xattn, g_ffn = _rec_inputs()

    def _L0_xattn_setup():
        import jax, jax.numpy as jnp
        import numpy as np
        HIDDEN = 256
        HEADS = 16
        HEAD_DIM = HIDDEN // HEADS
        SCALE = 1.0 / np.sqrt(HEAD_DIM).astype(np.float32)
        key = jax.random.key(seed)
        ks = jax.random.split(key, 8)
        b, t = (2, 512)
        x = jax.random.normal(ks[0], (b, t, HIDDEN), dtype=jnp.float32)
        context = x
        s = 0.02
        Wq = jax.random.normal(ks[1], (HIDDEN, HIDDEN), dtype=jnp.float32) * s
        Wk = jax.random.normal(ks[2], (HIDDEN, HIDDEN), dtype=jnp.float32) * s
        Wv = jax.random.normal(ks[3], (HIDDEN, HIDDEN), dtype=jnp.float32) * s
        Wo = jax.random.normal(ks[4], (HIDDEN, HIDDEN), dtype=jnp.float32) * s
        bo = jnp.zeros((HIDDEN,), dtype=jnp.float32)
        return {'x': x, 'context': context, 'Wq': Wq, 'Wk': Wk, 'Wv': Wv, 'Wo': Wo, 'bo': bo}
    _L0_xattn_all = _L0_xattn_setup()
    _L0_xattn_in = {k: v for k, v in _L0_xattn_all.items() if k in ('Wq', 'Wk', 'Wv', 'Wo', 'bo')}
    del _L0_xattn_all

    def _L0_ffn_setup():
        import jax, jax.numpy as jnp
        import numpy as np
        CAPACITY = 2
        B, S, D, E, I = (4, 1024, 256, 8, 1024)
        key = jax.random.key(seed)
        k0, k1, k2, k3, k4 = jax.random.split(key, 5)
        x = jax.random.normal(k0, (B, S, D), dtype=jnp.float32)
        gate_w = jax.random.normal(k1, (E, D), dtype=jnp.float32) * 0.006
        w_gate = jax.random.normal(k2, (E, I, D), dtype=jnp.float32) * (1.0 / np.sqrt(D))
        w_up = jax.random.normal(k3, (E, I, D), dtype=jnp.float32) * (1.0 / np.sqrt(D))
        w_down = jax.random.normal(k4, (E, D, I), dtype=jnp.float32) * (1.0 / np.sqrt(I))
        return {'x': x, 'gate_w': gate_w, 'w_gate': w_gate, 'w_up': w_up, 'w_down': w_down}
    _L0_ffn_all = _L0_ffn_setup()
    _L0_ffn_in = {k: v for k, v in _L0_ffn_all.items() if k in ('gate_w', 'w_gate', 'w_up', 'w_down')}
    del _L0_ffn_all
    return {'x': x, 'ctx_1024': ctx_1024, 'g_xattn': g_xattn, 'g_ffn': g_ffn, 'L0_xattn_Wq': _L0_xattn_in['Wq'], 'L0_xattn_Wk': _L0_xattn_in['Wk'], 'L0_xattn_Wv': _L0_xattn_in['Wv'], 'L0_xattn_Wo': _L0_xattn_in['Wo'], 'L0_xattn_bo': _L0_xattn_in['bo'], 'L0_ffn_gate_w': _L0_ffn_in['gate_w'], 'L0_ffn_w_gate': _L0_ffn_in['w_gate'], 'L0_ffn_w_up': _L0_ffn_in['w_up'], 'L0_ffn_w_down': _L0_ffn_in['w_down']}

def reference(x, ctx_1024, g_xattn, g_ffn, L0_xattn_Wq, L0_xattn_Wk, L0_xattn_Wv, L0_xattn_Wo, L0_xattn_bo, L0_ffn_gate_w, L0_ffn_w_gate, L0_ffn_w_up, L0_ffn_w_down):
    import jax
    import jax.numpy as jnp

    def _L0_xattn_ref(x, context, Wq, Wk, Wv, Wo, bo):
        import jax, jax.numpy as jnp
        import numpy as np
        HIDDEN = 256
        HEADS = 16
        HEAD_DIM = HIDDEN // HEADS
        SCALE = 1.0 / np.sqrt(HEAD_DIM).astype(np.float32)
        b, t, c = x.shape
        kv_t = context.shape[1]
        q = x @ Wq.T
        k = context @ Wk.T
        v = context @ Wv.T
        q = q.reshape(b, t, HEADS, HEAD_DIM).transpose(0, 2, 1, 3)
        k = k.reshape(b, kv_t, HEADS, HEAD_DIM).transpose(0, 2, 1, 3)
        v = v.reshape(b, kv_t, HEADS, HEAD_DIM).transpose(0, 2, 1, 3)
        scores = jnp.einsum('bhqd,bhkd->bhqk', q, k) * SCALE
        causal = jnp.tril(jnp.ones((t, kv_t), dtype=bool))
        scores = jnp.where(causal[None, None, :, :], scores, -jnp.inf)
        probs = jax.nn.softmax(scores, axis=-1)
        y = jnp.einsum('bhqk,bhkd->bhqd', probs, v)
        y = y.transpose(0, 2, 1, 3).reshape(b, t, c)
        return y @ Wo.T + bo

    def _L0_ffn_ref(x, gate_w, w_gate, w_up, w_down):
        import jax, jax.numpy as jnp
        import numpy as np
        CAPACITY = 2
        B, S, D = x.shape
        E = gate_w.shape[0]
        k = S // E * CAPACITY
        logits = jnp.einsum('bsd,ed->bse', x, gate_w)
        affinity = jax.nn.softmax(logits, axis=-1)
        affinity = jnp.transpose(affinity, (0, 2, 1))
        gating, idx = jax.lax.top_k(affinity, k)
        bidx = jnp.arange(B)[:, None, None]
        x_in = x[bidx, idx]
        h = jax.nn.silu(jnp.einsum('bekd,eid->beki', x_in, w_gate)) * jnp.einsum('bekd,eid->beki', x_in, w_up)
        x_e = jnp.einsum('beki,edi->bekd', h, w_down)
        out = jnp.zeros_like(x).at[bidx, idx].add(gating[..., None] * x_e)
        return out
    x = x + jnp.tanh(g_xattn[0]) * _L0_xattn_ref(_layernorm(x, axis=-1), ctx_1024, L0_xattn_Wq, L0_xattn_Wk, L0_xattn_Wv, L0_xattn_Wo, L0_xattn_bo)
    x = x + jnp.tanh(g_ffn[0]) * _L0_ffn_ref(_layernorm(x, axis=-1), L0_ffn_gate_w, L0_ffn_w_gate, L0_ffn_w_up, L0_ffn_w_down)
    return x

_drawn_inputs = setup_inputs


def setup_inputs(seed=0):
    import zlib

    import numpy as np

    out = dict(_drawn_inputs(seed))
    spreads = {'L0_xattn_bo': (0.0, 0.1)}
    factors = {'L0_xattn_Wq': 8.0, 'L0_xattn_Wk': 8.0}
    for name, (base, spread) in spreads.items():
        noise = np.random.default_rng([zlib.crc32(name.encode()), seed]).standard_normal(out[name].shape)
        drawn = base * np.exp(spread * noise) if base else spread * noise
        out[name] = jnp.asarray(drawn.astype(out[name].dtype))
    for name, factor in factors.items():
        out[name] = (out[name] * factor).astype(out[name].dtype)
    return out
```

```python
from contextlib import ExitStack

import concourse.bass as bass
from concourse import mybir

ALU = mybir.AluOpType
ACT = mybir.ActivationFunctionType
AX = mybir.AxisListType
F32 = mybir.dt.float32
BF16 = mybir.dt.bfloat16
U32 = mybir.dt.uint32

P = 128
BATCH = 16
T = 512
D = 256
HEADS = 16
HD = D // HEADS
NT = T // P
NH2 = D // P
GROUPS = 4
GH = HEADS // GROUPS
EXPERTS = 8
SLOTS = T // EXPERTS * 2
INNER = 1024
EPS = 1e-5
NEG = -1e30

STACK = 6 * HD
ROWS = STACK + 2

MAX_UNITS = [(0, 0, 4), (1, 0, 2), (1, 2, 2)] + [(i, h, 1) for i in (2, 3) for h in range(GH)]
NMAX = len(MAX_UNITS)
SC_UNITS = []
for _h in (0, 2):
    SC_UNITS += [(_h, 1, (0,)), (_h, 1, (1, 3)), (_h + 1, 1, (0,)), (_h + 1, 1, (1, 3)), (_h, 2, (2,))]
NSC = len(SC_UNITS)
SC_BANK = [0, 1, 2, 0, 1, 2, 0, 1, 2, 1]
SC_BEFORE = [6 - NSC, 9 - NSC, 8 - NSC, 0, 1, 2, 3, 4, 5, 7]
PWIDTH = [T - P * j for j in range(NT)]
POFF = [0, 512, 1024, 896]
PALL = sum(PWIDTH)


def steps(body, jobs_only=False):
    b = body
    order = []
    extra = {
        0: {0: [("ln1", b + 1)], 1: [("yt", b - 1, 0)], 2: [("yt+", b - 1, 0), ("yb", b - 2, 1)],
            3: [("yb+", b - 2, 1), ("ln1+", b + 1)], 4: [("o", b - 2, 0), ("o+", b - 2, 0)],
            5: [("o", b - 2, 1), ("o+", b - 2, 1)],
            6: [("tx", b + 1, 0), ("tx+", b + 1, 0), ("ln2", b - 2)],
            7: [("tx", b + 1, 1), ("tx+", b + 1, 1)],
            8: [("tc", b + 1, 0), ("tc+", b + 1, 0), ("ln2+", b - 2)],
            9: [("tc", b + 1, 1), ("tc+", b + 1, 1)], 10: [("mt", b, 0)]},
        1: {0: [("mt+", b, 0), ("stack", b, 2)], 1: [("yt", b - 1, 1)], 2: [("yt+", b - 1, 1)],
            4: [("q", b + 1, 0), ("q+", b + 1, 0)], 6: [("q", b + 1, 1), ("q+", b + 1, 1)],
            7: [("xs", b - 2), ("mrow", b, 0)], 10: [("mt", b, 1)]},
        2: {0: [("mt+", b, 1), ("stack", b, 3), ("qstore", b + 1)], 1: [("yt", b - 1, 2)],
            2: [("yt+", b - 1, 2)],
            3: [("yb", b - 1, 0), ("yb+", b - 1, 0)], 4: [("k", b + 1, 0), ("k+", b + 1, 0)],
            6: [("k", b + 1, 1), ("k+", b + 1, 1)], 7: [("mrow", b, 1)],
            8: [("xt", b - 2, 0), ("xt+", b - 2, 0), ("res", b - 1)],
            9: [("xt", b - 2, 1), ("xt+", b - 2, 1), ("vaug", b)],
            10: [("mt", b, 2)]},
        3: {0: [("mt+", b, 2), ("kstore", b + 1)], 1: [("yt", b - 1, 3), ("load", b + 2)],
            2: [("yt+", b - 1, 3)], 3: [("ll", b - 2), ("ll+", b - 2)],
            4: [("mrow", b, 2), ("v", b + 1, 0), ("v+", b + 1, 0)],
            6: [("v", b + 1, 1), ("v+", b + 1, 1), ("stack", b + 1, 0)],
            8: [("save", b - 2)], 10: [("mt", b, 3), ("mt+", b, 3), ("stack", b + 1, 1)]},
    }
    for g in range(GROUPS):
        sc = (b, g - 2) if g >= 2 else (b - 1, g + 2)
        pv = (b, g - 3) if g >= 3 else (b - 1, g + 1)
        for k in range(NMAX):
            if g == 0 and k == 4:
                order.append(("mrow", b - 1, 3))
            order.append(("max", b, g, k))
            if k < NSC:
                order.append(("sc", *sc, k))
            if k in (1, 3, 5, 7):
                order.append(("pv", *pv, k // 2))
            if k == 8:
                order.append(("pv+", *pv))
            order += extra[g].get(k, [])
    return [p for p in order if not isinstance(p[1], int) or 0 <= p[1] < BATCH]


JOB_BANK = {("yt", 0): 0, ("yb", 1): 1, ("o", 0): 0, ("o", 1): 1, ("tx", 0): 0, ("tx", 1): 1, ("tc", 0): 0,
            ("tc", 1): 1, ("mt", 0): 0,
            ("yt", 1): 1, ("q", 0): 0, ("q", 1): 1, ("mt", 1): 0,
            ("yt", 2): 1, ("yb", 0): 0, ("k", 0): 1, ("k", 1): 0, ("xt", 0): 1, ("xt", 1): 0, ("mt", 2): 1,
            ("yt", 3): 0, ("ll", 0): 1, ("v", 0): 0, ("v", 1): 1, ("mt", 3): 0}
JOBS_A_BATCH = {"yt": 4, "yb": 2, "o": 2, "tx": 2, "tc": 2, "mt": 4, "q": 2, "k": 2, "xt": 2, "ll": 1, "v": 2}


def key(p):
    return (p[0], p[2] if len(p) > 2 else 0)


def count(b, per, k):
    return b * per + k


def wait(eng, s, value):
    if not isinstance(value, int) or value > 0:
        eng.wait_ge(s, value)


def wait_apart(eng, s, value, passed):
    wait(eng, s, value)
    if not isinstance(value, int):
        eng.sem_inc(passed, 1)


def flamingo(nc, x, ctx_kv, g_xattn, g_ffn, wq, wk, wv, wo, bo, gate_w, w_gate, w_up, w_down, out):
    with ExitStack() as stack:
        def sem(name):
            return stack.enter_context(nc.semaphore(name))

        def sb(ctx, name, shape, dt):
            return ctx.enter_context(nc.sbuf_tensor(name, shape, dt))

        bank = [stack.enter_context(nc.psum_tensor(f"bank{i}", [P, 512], F32)) for i in range(8)]
        max_bank, sc_bank, pv_bank, job_bank = bank[0:2], bank[2:5], bank[5], bank[6:8]

        q_dram = nc.dram_tensor("q_parts", [BATCH, GROUPS, 3, HD * GH, T], BF16, kind="Internal").ap()
        k_dram = nc.dram_tensor("k_parts", [BATCH, GROUPS, 3, HD * GH, T], BF16, kind="Internal").ap()
        m_dram = nc.dram_tensor("m_parts", [BATCH, GROUPS, 2, GH * NT, P], BF16, kind="Internal").ap()
        tok_dram = nc.dram_tensor("tokens", [BATCH * T, 2 * D], BF16, kind="Internal").ap()

        ident = sb(stack, "ident", [P, P], F32)
        identb = sb(stack, "identb", [P, P], BF16)
        aff = sb(stack, "aff", [P, NT, EXPERTS * BATCH], F32)
        tanh_g = sb(stack, "tanh_g", [P, 2], F32)
        passed = {n: sem(f"passed_{n}") for n in ("dve", "pool", "sp")}

        with ExitStack() as ctx:
            attention(nc, ctx, stack, sb, sem, locals())
        with ExitStack() as ctx:
            experts(nc, ctx, sb, sem, locals())


def attention(nc, ctx, stack, sb, sem, g):
    x, ctx_kv, out = g["x"], g["ctx_kv"], g["out"]
    ident, identb, aff, tanh_g, passed = g["ident"], g["identb"], g["aff"], g["tanh_g"], g["passed"]
    max_bank, sc_bank, pv_bank, job_bank = g["max_bank"], g["sc_bank"], g["pv_bank"], g["job_bank"]
    q_dram, k_dram, m_dram, tok_dram = g["q_dram"], g["k_dram"], g["m_dram"], g["tok_dram"]

    mask_qk = sb(ctx, "mask_qk", [P, P], BF16)
    mask_kq = sb(ctx, "mask_kq", [P, P], BF16)
    wT = {n: sb(ctx, f"{n}T", [P, NH2, D], F32) for n in ("wq", "wk", "wv", "wo")}
    gwT = sb(ctx, "gwT", [P, NH2, EXPERTS], F32)
    bias = sb(ctx, "bias", [P, D], F32)
    minus_half = sb(ctx, "minus_half", [P, NT], F32)

    x_t = sb(ctx, "x_t", [P, NT, D], F32)
    ctx_t = sb(ctx, "ctx_t", [P, NT, D], F32)
    res_t = sb(ctx, "res_t", [P, NT, D], F32)
    xn = sb(ctx, "xn", [P, NT, D], F32)
    xT = sb(ctx, "xT", [P, NH2, T], F32)
    cT = sb(ctx, "cT", [P, NH2, T], F32)
    parts = {"q": sb(ctx, "q_sb", [P, 3, NH2, T], BF16), "k": sb(ctx, "k_sb", [P, 3, NH2, T], BF16)}
    rest = sb(ctx, "rest", [P, 2, T], F32)
    qs = sb(ctx, "qs", [ROWS, GROUPS, GH, T], BF16)
    ks = sb(ctx, "ks", [ROWS, GROUPS, GH, T], BF16)
    prob = sb(ctx, "prob", [P, 2, GH, PALL], F32)
    v_new = sb(ctx, "v_new", [P, NT, D], F32)
    v_aug = sb(ctx, "v_aug", [P, NT, HEADS, 32], F32)
    mx = sb(ctx, "mx", [P, 2, GH, NT], F32)
    m_parts = sb(ctx, "m_sb", [GH * NT, 2, P], BF16)
    yT = sb(ctx, "yT", [P, T], F32)
    rden = sb(ctx, "rden", [P, NT, GH, 1], F32)
    yq = sb(ctx, "yq", [P, NT, D], F32)
    ynT = sb(ctx, "ynT", [P, NH2, T], F32)
    x1 = sb(ctx, "x1", [P, NT, D], F32)
    xn2 = sb(ctx, "xn2", [P, NT, D], F32)
    tok = sb(ctx, "tok", [P, NT, 2 * D], BF16)
    xn2T = sb(ctx, "xn2T", [P, NH2, T], F32)
    stats = {n: sb(ctx, f"{n}_stats", [P, NT, 6], F32) for n in ("ln1", "ln2")}
    mean_var = {n: sb(ctx, f"{n}_mv", [P, NT, 2], F32) for n in ("ln1", "ln2")}
    var_eps = {n: sb(ctx, f"{n}_ve", [P, NT], F32) for n in ("ln1", "ln2")}
    rstd = {n: sb(ctx, f"{n}_rstd", [P, NT], F32) for n in ("ln1", "ln2")}
    lmax = sb(ctx, "lmax", [P, NT, 1], F32)
    logit = sb(ctx, "logit", [P, NT, EXPERTS], F32)
    lexp = sb(ctx, "lexp", [P, NT, EXPERTS], F32)
    lsum = sb(ctx, "lsum", [P, NT, 1], F32)
    lrec = sb(ctx, "lrec", [P, NT, 1], F32)

    with ExitStack() as tmp:
        w_raw = {n: sb(tmp, f"{n}_raw", [P, NH2, D], F32) for n in ("wq", "wk", "wv", "wo")}
        gw_raw = sb(tmp, "gw_raw", [EXPERTS, D], F32)
        gates = sb(tmp, "gates", [P, 2], F32)
        bo_rep = sb(tmp, "bo_rep", [P, D], F32)
        loaded, gates_loaded, consts, cast, turned, evac, tanh_done, bias_done = (
            sem(n) for n in ("loaded", "gates_loaded", "consts", "cast", "turned", "evac", "tanh_done", "bias_done"))
        order = [(n, o) for n in ("wq", "wk", "wv", "wo") for o in range(NH2)]
        with nc.Block() as block:
            @block.sync
            def _(sp):
                for n in ("wq", "wk", "wv", "wo"):
                    sp.dma_start(w_raw[n][:, :, :], g[n].rearrange("(o p) i -> p o i", p=P)).then_inc(loaded, 16)
                sp.dma_start(gw_raw[:, :], g["gate_w"]).then_inc(loaded, 16)
                sp.dma_start(bo_rep[:, :], g["bo"].partition_broadcast(P)).then_inc(gates_loaded, 16)
                sp.dma_start(gates[:, 0:1], g["g_xattn"].partition_broadcast(P)).then_inc(gates_loaded, 16)
                sp.dma_start(gates[:, 1:2], g["g_ffn"].partition_broadcast(P)).then_inc(gates_loaded, 16)

            @block.gpsimd
            def _(pool):
                nc.gpsimd.memset(ident[:, :], 0.0).then_inc(consts, 1)
                nc.gpsimd.memset(mask_qk[:, :], 0.0).then_inc(consts, 1)
                nc.gpsimd.memset(mask_kq[:, :], 0.0).then_inc(consts, 1)
                nc.gpsimd.memset(minus_half[:, :], -0.5).then_inc(consts, 1)
                nc.gpsimd.memset(v_aug[:, :, :, :], 1.0).then_inc(consts, 1)
                pool.wait_ge(consts, 5)
                nc.gpsimd.affine_select(out=ident[:, :], in_=ident[:, :], compare_op=ALU.not_equal, fill=1.0,
                                        base=0, pattern=[[-1, P]], channel_multiplier=1).then_inc(consts, 1)
                nc.gpsimd.affine_select(out=mask_qk[:, :], in_=mask_qk[:, :], compare_op=ALU.is_ge, fill=NEG,
                                        base=0, pattern=[[-1, P]], channel_multiplier=1).then_inc(consts, 1)
                nc.gpsimd.affine_select(out=mask_kq[:, :], in_=mask_kq[:, :], compare_op=ALU.is_ge, fill=NEG,
                                        base=0, pattern=[[1, P]], channel_multiplier=-1).then_inc(consts, 1)

            @block.vector
            def _(dve):
                nc.vector.memset(ks[STACK:ROWS, :, :, :], 1.0).then_inc(cast, 1)
                dve.wait_ge(consts, 8)
                nc.vector.tensor_copy(identb[:, :], ident[:, :]).then_inc(cast, 1)
                dve.wait_ge(gates_loaded, 48)
                dve.wait_ge(tanh_done, 1)
                nc.vector.tensor_scalar(bias[:, :], bo_rep[:, :], tanh_g[:, 0:1], None, ALU.mult).then_inc(bias_done, 1)

            @block.tensor
            def _(pe):
                pe.wait_ge(loaded, 80)
                pe.wait_ge(consts, 8)
                for n, (name, o) in enumerate(order):
                    if n >= 2:
                        pe.wait_ge(evac, n - 1)
                    for i in range(NH2):
                        last = nc.tensor.transpose(job_bank[n % 2][:, i * P:(i + 1) * P],
                                                   w_raw[name][:, o, i * P:(i + 1) * P], ident[:, :])
                    last.then_inc(turned, 1)
                n = len(order)
                pe.wait_ge(evac, n - 1)
                for i in range(NH2):
                    last = nc.tensor.transpose(job_bank[n % 2][:, i * EXPERTS:(i + 1) * EXPERTS],
                                               gw_raw[:, i * P:(i + 1) * P], ident[0:EXPERTS, 0:EXPERTS])
                last.then_inc(turned, 1)

            @block.scalar
            def _(act):
                act.wait_ge(gates_loaded, 48)
                nc.scalar.activation(tanh_g[:, :], gates[:, :], ACT.Tanh).then_inc(tanh_done, 1)
                for n, (name, o) in enumerate(order):
                    act.wait_ge(turned, n + 1)
                    for i in range(NH2):
                        dst, src = wT[name][:, i, o * P:(o + 1) * P], job_bank[n % 2][:, i * P:(i + 1) * P]
                        if name in ("wq", "wk"):
                            dst = dst.rearrange("p (g d h) -> p g h d", g=2, h=GH)
                            src = src.rearrange("p (g h d) -> p g h d", g=2, h=GH)
                        last = nc.scalar.activation(dst, src, ACT.Copy)
                    last.then_inc(evac, 1)
                n = len(order)
                act.wait_ge(turned, n + 1)
                nc.scalar.activation(gwT[:, :, :], job_bank[n % 2][:, 0:NH2 * EXPERTS].rearrange(
                    "p (i c) -> p i c", i=NH2), ACT.Copy).then_inc(evac, 1)

    x_loaded, ctx_loaded, res_loaded = sem("x_loaded"), sem("ctx_loaded"), sem("res_loaded")
    stack_loaded = [sem(f"stack_loaded{i}") for i in range(GROUPS)]
    mrow_loaded = [sem(f"mrow_loaded{i}") for i in range(GROUPS)]
    stored = {n: sem(f"{n}_stored") for n in ("q", "k")}
    mrow_stored, x1_stored, tok_stored = sem("mrow_stored"), sem("x1_stored"), sem("tok_stored")
    filled = {n: sem(f"{n}_filled") for n in JOBS_A_BATCH}
    read = {n: sem(f"{n}_read") for n in JOBS_A_BATCH}
    hi_done = {n: sem(f"{n}_hi_done") for n in ("q", "k", "mt")}
    rest_split = sem("rest_split")
    max_filled, max_read = sem("max_filled"), sem("max_read")
    sc_filled, exp_done = sem("sc_filled"), sem("exp_done")
    pv_filled, pv_read = sem("pv_filled"), sem("pv_read")
    rden_done, vaug_done, res_done = sem("rden_done"), sem("vaug_done"), sem("res_done")
    ln_stats = {n: sem(f"{n}_stats_done") for n in ("ln1", "ln2")}
    ln_aggr = {n: sem(f"{n}_aggr_done") for n in ("ln1", "ln2")}
    ln_var = {n: sem(f"{n}_var_done") for n in ("ln1", "ln2")}
    ln_rstd = {n: sem(f"{n}_rstd_done") for n in ("ln1", "ln2")}
    ln_done = {n: sem(f"{n}_done") for n in ("ln1", "ln2")}
    tok_hi, tok_lo = sem("tok_hi"), sem("tok_lo")
    lmax_done, lexp_done, lsum_done, lrec_done, aff_done = (
        sem(n) for n in ("lmax_done", "lexp_done", "lsum_done", "lrec_done", "aff_done"))

    def rounds(eng, body):
        for b in (-1, 0, 1, 2):
            for p in steps(b):
                body(b, p)
        with eng.Fori(3, BATCH - 2) as b:
            for p in steps(b):
                body(b, p)
        for b in range(BATCH - 2, BATCH + 2):
            for p in steps(b):
                body(b, p)

    def free_bank(pe, b, p):
        mine = JOB_BANK[key(p)]
        jobs = [q for q in steps(b) if key(q) in JOB_BANK and JOB_BANK[key(q)] == mine]
        at = [key(q) for q in jobs].index(key(p))
        if at:
            q = jobs[at - 1]
        else:
            q = [q for q in steps(b - 1) if key(q) in JOB_BANK and JOB_BANK[key(q)] == mine]
            if not q:
                return
            q = q[-1]
        wait(pe, read[q[0]], count(q[1], JOBS_A_BATCH[q[0]], key(q)[1] + 1))

    with nc.Block() as block:
        @block.sync
        def _(sp):
            def hold(s, value):
                wait_apart(sp, s, value, passed["sp"])

            def load(b):
                hold(ln_done["ln1"], count(b, NT, 0))
                sp.dma_start(x_t[:, :, :], x[b].rearrange("(i p) d -> p i d", p=P)).then_inc(x_loaded, 16)
                hold(filled["tc"], count(b, NH2, 0))
                sp.dma_start(ctx_t[:, :, :], ctx_kv[b][0:T, :].rearrange("(i p) d -> p i d", p=P)).then_inc(ctx_loaded, 16)

            def piece(body, p):
                kind, b = p[0], p[1]
                if kind == "load":
                    load(b)
                elif kind == "res":
                    hold(read["o"], count(b, 2, 0))
                    sp.dma_start(res_t[:, :, :], x[b].rearrange("(i p) d -> p i d", p=P)).then_inc(res_loaded, 16)
                elif kind in ("qstore", "kstore"):
                    n = kind[0]
                    hold(rest_split, count(b, 4, 2 if n == "q" else 4))
                    dram = (q_dram if n == "q" else k_dram)[b]
                    for r in range(3):
                        for t in range(NH2):
                            sp.dma_start(dram[2 * t:2 * t + 2, r, :, :], parts[n][:, r, t, :]).then_inc(stored[n], 16)
                elif kind == "stack":
                    gr = p[2]
                    hold(stored["q"], count(b, 96, 96))
                    hold(stored["k"], count(b, 96, 96))
                    hold(sc_filled, count(b, GROUPS * NSC, (gr + 1 - GROUPS) * NSC))
                    at = 0
                    for r in (3, 2, 1):
                        src = q_dram[b][gr][0:r].rearrange("r (d h) t -> (r d) (h t)", h=GH)
                        sp.dma_start(qs[at:at + r * HD, gr, :, :].rearrange("p h t -> p (h t)"), src)\
                            .then_inc(stack_loaded[gr], 16)
                        src = k_dram[b][gr][3 - r:4 - r].rearrange("r (d h) t -> r d (h t)", h=GH)
                        src = src.broadcast_to([r, HD, GH * T])
                        sp.dma_start(ks[at:at + r * HD, gr, :, :].rearrange("p h t -> p (h t)"), src)\
                            .then_inc(stack_loaded[gr], 16)
                        at += r * HD
                elif kind == "mrow":
                    gr = p[2]
                    n = count(b, GROUPS, gr)
                    hold(read["mt"], n + 1)
                    sp.dma_start(m_dram[b][gr].rearrange("r a q -> a r q"), m_parts[:, :, :]).then_inc(mrow_stored, 16)
                    hold(mrow_stored, n * 16 + 16)
                    hold(sc_filled, count(b, GROUPS * NSC, (gr + 1 - GROUPS) * NSC))
                    sp.dma_start(qs[STACK:ROWS, gr, :, :], m_dram[b][gr].rearrange("r (h i) q -> r h (i q)", h=GH))\
                        .then_inc(mrow_loaded[gr], 16)
                elif kind == "save":
                    hold(ln_stats["ln2"], count(b, NT, NT))
                    sp.dma_start(out[b].rearrange("(i p) d -> p i d", p=P), x1[:, :, :]).then_inc(x1_stored, 16)
                    hold(tok_lo, count(b, 1, 1))
                    if isinstance(b, int):
                        dst = tok_dram[b * T:(b + 1) * T, :]
                    else:
                        dst = tok_dram[bass.ts(b, T), :]
                    sp.dma_start(dst.rearrange("(i p) d -> p i d", p=P), tok[:, :, :]).then_inc(tok_stored, 16)

            load(0)
            rounds(sp, piece)
            sp.wait_ge(x1_stored, 16 * BATCH)
            sp.wait_ge(tok_stored, 16 * BATCH)

        @block.tensor
        def _(pe):
            def piece(body, p):
                kind, b = p[0], p[1]
                if key(p) in JOB_BANK:
                    free_bank(pe, body, p)
                    to = job_bank[JOB_BANK[key(p)]]
                if kind == "max":
                    gr, k = p[2], p[3]
                    i, h0, nh = MAX_UNITS[k]
                    n = count(b, GROUPS * NMAX, gr * NMAX + k)
                    if k == 0:
                        wait(pe, stack_loaded[gr], count(b, 96, 96))
                    wait(pe, max_read, n - 1)
                    w = P * (i + 1)
                    dst = max_bank[(gr * NMAX + k) % 2]
                    for h in range(nh):
                        nc.tensor.matmul(dst[:, h * w:(h + 1) * w], qs[0:STACK, gr, h0 + h, i * P:(i + 1) * P],
                                         ks[0:STACK, gr, h0 + h, 0:w], start=True, stop=False)
                        last = nc.tensor.matmul(dst[:, h * w + w - P:(h + 1) * w], identb[:, :], mask_qk[:, :],
                                                start=False, stop=True)
                    last.then_inc(max_filled, 1)
                elif kind == "sc":
                    gr, k = p[2], p[3]
                    h0, nh, tiles = SC_UNITS[k]
                    if k == 0:
                        wait(pe, mrow_loaded[gr], count(b, 16, 16))
                    wait(pe, exp_done, count(b, GROUPS * NSC, gr * NSC + SC_BEFORE[k] + 1))
                    at = 0
                    for h in range(nh):
                        for j in tiles:
                            dst = sc_bank[SC_BANK[k]]
                            nc.tensor.matmul(dst[:, at:at + PWIDTH[j]], ks[:, gr, h0 + h, j * P:(j + 1) * P],
                                             qs[:, gr, h0 + h, j * P:T], start=True, stop=False)
                            last = nc.tensor.matmul(dst[:, at:at + P], identb[:, :], mask_kq[:, :],
                                                    start=False, stop=True)
                            at += PWIDTH[j]
                    last.then_inc(sc_filled, 1)
                elif kind == "pv":
                    gr, j = p[2], p[3]
                    n = count(b, GROUPS, gr)
                    if j == 0:
                        wait(pe, exp_done, (n + 1) * NSC)
                        wait(pe, vaug_done, count(b, 1, 1))
                        wait(pe, pv_read, n)
                    for h in range(GH):
                        last = nc.tensor.matmul(pv_bank[32 * h:32 * h + 32, j * P:T], v_aug[:, j, gr * GH + h, :],
                                                prob[:, gr % 2, h, POFF[j]:POFF[j] + PWIDTH[j]],
                                                start=(j == 0), stop=(j == NT - 1))
                    if j == NT - 1:
                        last.then_inc(pv_filled, 1)
                elif kind == "mt":
                    gr = p[2]
                    wait(pe, max_read, count(b, GROUPS * NMAX, (gr + 1) * NMAX))
                    nc.tensor.transpose(to[0:GH * NT, 0:P], mx[:, gr % 2, :, :].rearrange("p h i -> p (h i)"),
                                        ident[:, :]).then_inc(filled[kind], 1)
                elif kind == "yt":
                    wait(pe, pv_read, count(b, GROUPS, p[2] + 1))
                    for i in range(NT):
                        last = nc.tensor.transpose(to[:, i * P:(i + 1) * P], yT[:, i * P:(i + 1) * P], ident[:, :])
                    last.then_inc(filled[kind], 1)
                elif kind in ("yb", "tx", "tc", "xt"):
                    half = p[2]
                    src = {"yb": yq, "tx": xn, "tc": ctx_t, "xt": xn2}[kind]
                    if kind == "yb":
                        wait(pe, read["yt"], count(b, GROUPS, 2 * half + 2))
                    elif kind == "tx":
                        wait(pe, ln_done["ln1"], count(b, NT, NT))
                    elif kind == "tc":
                        wait(pe, ctx_loaded, count(b, 16, 16))
                    else:
                        wait(pe, ln_done["ln2"], count(b, NT, NT))
                    for i in range(NT):
                        last = nc.tensor.transpose(to[:, i * P:(i + 1) * P], src[:, i, half * P:(half + 1) * P],
                                                   ident[:, :])
                    last.then_inc(filled[kind], 1)
                elif kind in ("q", "k"):
                    t = p[2]
                    src, made = (xT, "tx") if kind == "q" else (cT, "tc")
                    wait(pe, read[made], count(b, 2, 2))
                    for c in range(NH2):
                        last = nc.tensor.matmul(to[:, :], wT["w" + kind][:, c, t * P:(t + 1) * P], src[:, c, :],
                                                start=(c == 0), stop=(c == NH2 - 1))
                    last.then_inc(filled[kind], 1)
                elif kind in ("v", "o"):
                    src, made = (cT, "tc") if kind == "v" else (ynT, "yb")
                    wait(pe, read[made], count(b, 2, 2))
                    for i2 in range(2):
                        i = 2 * p[2] + i2
                        for c in range(NH2):
                            last = nc.tensor.matmul(to[:, i2 * D:(i2 + 1) * D], src[:, c, i * P:(i + 1) * P],
                                                    wT["w" + kind][:, c, :], start=(c == 0), stop=(c == NH2 - 1))
                    last.then_inc(filled[kind], 1)
                elif kind == "ll":
                    wait(pe, read["xt"], count(b, 2, 2))
                    for i in range(NT):
                        for c in range(NH2):
                            last = nc.tensor.matmul(to[:, i * EXPERTS:(i + 1) * EXPERTS],
                                                    xn2T[:, c, i * P:(i + 1) * P], gwT[:, c, :],
                                                    start=(c == 0), stop=(c == NH2 - 1))
                    last.then_inc(filled[kind], 1)

            rounds(pe, piece)

        @block.scalar
        def _(act):
            def piece(body, p):
                kind, b = p[0], p[1]
                job = kind[:-1] if kind.endswith("+") else None
                if job and (job, key(p)[1]) in JOB_BANK:
                    src = job_bank[JOB_BANK[(job, key(p)[1])]]
                if kind == "sc":
                    gr, k = p[2], p[3]
                    h0, nh, tiles = SC_UNITS[k]
                    n = count(b, GROUPS, gr)
                    if k == 0:
                        wait(act, pv_filled, n - 1)
                    wait(act, sc_filled, n * NSC + k + 1)
                    w = sum(PWIDTH[j] for j in tiles)
                    nc.scalar.activation(prob[:, gr % 2, h0:h0 + nh, POFF[tiles[0]]:POFF[tiles[0]] + w],
                                         sc_bank[SC_BANK[k]][:, 0:nh * w].rearrange("p (h w) -> p h w", h=nh),
                                         ACT.Exp, scale=float(HD) ** -0.5).then_inc(exp_done, 1)
                elif kind == "pv+":
                    n = count(b, GROUPS, p[2])
                    wait(act, pv_filled, n + 1)
                    wait(act, filled["yt"], n)
                    nc.scalar.activation(yT[:, :], pv_bank[:, :], ACT.Copy).then_inc(pv_read, 1)
                elif kind == "mt+":
                    n = count(b, GROUPS, p[2])
                    wait(act, filled["mt"], n + 1)
                    wait(act, mrow_stored, n * 16)
                    nc.scalar.activation(m_parts[:, 0, :], src[0:GH * NT, 0:P], ACT.Copy, scale=-1.0)\
                        .then_inc(hi_done["mt"], 1)
                elif kind in ("tx+", "tc+", "yb+", "xt+"):
                    half = p[2]
                    dst, user, per = {"tx": (xT, "q", 2), "tc": (cT, "v", 2), "yb": (ynT, "o", 2),
                                      "xt": (xn2T, "ll", 1)}[job]
                    wait(act, filled[job], count(b, 2, half + 1))
                    wait(act, filled[user], count(b, per, 0))
                    nc.scalar.activation(dst[:, half, :], src[:, :], ACT.Copy).then_inc(read[job], 1)
                elif kind in ("q+", "k+"):
                    t = p[2]
                    wait(act, filled[job], count(b, 2, t + 1))
                    wait(act, stored[job], count(b, 96, 0))
                    nc.scalar.activation(parts[job][:, 0, t, :], src[:, :], ACT.Copy).then_inc(hi_done[job], 1)
                elif kind == "v+":
                    wait(act, filled["v"], count(b, 2, p[2] + 1))
                    wait(act, vaug_done, count(b, 1, 0))
                    nc.scalar.activation(v_new[:, 2 * p[2]:2 * p[2] + 2, :],
                                         src[:, :].rearrange("p (i d) -> p i d", i=2), ACT.Copy).then_inc(read["v"], 1)
                elif kind == "ll+":
                    wait(act, read["ll"], count(b, 1, 1))
                    wait(act, aff_done, count(b, 1, 0))
                    nc.scalar.activation(lexp[:, :, :], logit[:, :, :], ACT.Exp).then_inc(lexp_done, 1)

            rounds(act, piece)

        @block.vector
        def _(dve):
            def norm_stats(n, src, b):
                for i in range(NT):
                    nc.vector.bn_stats(stats[n][:, i, :], src[:, i, :]).then_inc(ln_stats[n], 1)
                wait_apart(dve, ln_stats[n], count(b, NT, NT), passed["dve"])
                for i in range(NT):
                    nc.vector.bn_aggr(mean_var[n][:, i, :], stats[n][:, i, :]).then_inc(ln_aggr[n], 1)
                wait(dve, ln_aggr[n], count(b, NT, NT))
                wait(dve, ln_rstd[n], count(b, 1, 0))
                nc.vector.tensor_scalar_add(var_eps[n][:, :], mean_var[n][:, :, 1], EPS).then_inc(ln_var[n], 1)

            def norm_apply(n, dst, src, b):
                wait(dve, ln_rstd[n], count(b, 1, 1))
                for i in range(NT):
                    nc.vector.tensor_scalar(dst[:, i, :], src[:, i, :], mean_var[n][:, i, 0:1],
                                            rstd[n][:, i:i + 1], ALU.subtract, ALU.mult).then_inc(ln_done[n], 1)

            def piece(body, p):
                kind, b = p[0], p[1]
                job = kind[:-1] if kind.endswith("+") else None
                if job and (job, key(p)[1]) in JOB_BANK:
                    src = job_bank[JOB_BANK[(job, key(p)[1])]]
                if kind == "max":
                    gr, k = p[2], p[3]
                    i, h0, nh = MAX_UNITS[k]
                    w = P * (i + 1)
                    if k == 0:
                        wait(dve, filled["mt"], count(b, GROUPS, gr - 1))
                    wait(dve, max_filled, count(b, GROUPS * NMAX, gr * NMAX + k + 1))
                    nc.vector.tensor_reduce(mx[:, gr % 2, h0:h0 + nh, i], max_bank[(gr * NMAX + k) % 2][
                        :, 0:nh * w].rearrange("p (h w) -> p h w", h=nh), AX.X, ALU.max).then_inc(max_read, 1)
                elif kind == "mt+":
                    wait(dve, hi_done["mt"], count(b, GROUPS, p[2] + 1))
                    nc.vector.scalar_tensor_tensor(m_parts[:, 1, :], src[0:GH * NT, 0:P], -1.0, m_parts[:, 0, :],
                                                   ALU.mult, ALU.subtract).then_inc(read["mt"], 1)
                elif kind in ("q+", "k+"):
                    t = p[2]
                    n = count(b, 4, t + (2 if job == "k" else 0))
                    wait(dve, hi_done[job], count(b, 2, t + 1))
                    wait(dve, rest_split, n - 1)
                    nc.vector.tensor_tensor(rest[:, t, :], src[:, :], parts[job][:, 0, t, :], ALU.subtract)\
                        .then_inc(read[job], 1)
                elif kind == "yt+":
                    gr = p[2]
                    n = count(b, GROUPS, gr + 1)
                    wait(dve, filled["yt"], n)
                    view = src[:, :].rearrange("p (i h c) -> p i h c", i=NT, h=GH)
                    nc.vector.reciprocal(rden[:, :, :, :], view[:, :, :, HD:HD + 1]).then_inc(rden_done, 1)
                    wait(dve, rden_done, n)
                    wait(dve, filled["yb"], count(b, 2, gr // 2 - 1))
                    nc.vector.tensor_tensor(
                        yq[:, :, gr * GH * HD:(gr + 1) * GH * HD].rearrange("p i (h d) -> p i h d", h=GH),
                        view[:, :, :, 0:HD], rden[:, :, :, :].broadcast_to([P, NT, GH, HD]), ALU.mult)\
                        .then_inc(read["yt"], 1)
                elif kind == "o+":
                    t = p[2]
                    wait(dve, filled["o"], count(b, 2, t + 1))
                    wait(dve, res_done, count(b, 1, 1))
                    if t == 0:
                        wait(dve, x1_stored, count(b, 16, 0))
                        wait(dve, ln_done["ln2"], count(b, NT, 0))
                    nc.vector.scalar_tensor_tensor(
                        x1[:, 2 * t:2 * t + 2, :], src[:, :].rearrange("p (i d) -> p i d", i=2), tanh_g[:, 0:1],
                        res_t[:, 2 * t:2 * t + 2, :], ALU.mult, ALU.add).then_inc(read["o"], 1)
                elif kind == "ln1":
                    wait(dve, x_loaded, count(b, 16, 16))
                    norm_stats("ln1", x_t, b)
                elif kind == "ln1+":
                    wait(dve, filled["tx"], count(b, 2, 0))
                    norm_apply("ln1", xn, x_t, b)
                elif kind == "ln2":
                    wait(dve, read["o"], count(b, 2, 2))
                    norm_stats("ln2", x1, b)
                elif kind == "ln2+":
                    wait(dve, filled["xt"], count(b, 2, 0))
                    wait(dve, tok_lo, count(b, 1, 0))
                    norm_apply("ln2", xn2, x1, b)
                elif kind == "ll+":
                    wait(dve, filled["ll"], count(b, 1, 1))
                    view = src[:, 0:NT * EXPERTS].rearrange("p (i e) -> p i e", i=NT)
                    nc.vector.tensor_reduce(lmax[:, :, 0], view, AX.X, ALU.max).then_inc(lmax_done, 1)
                    wait(dve, lmax_done, count(b, 1, 1))
                    wait(dve, lexp_done, count(b, 1, 0))
                    nc.vector.tensor_tensor(logit[:, :, :], view, lmax[:, :, :].broadcast_to([P, NT, EXPERTS]),
                                            ALU.subtract).then_inc(read["ll"], 1)
                    wait(dve, lexp_done, count(b, 1, 1))
                    nc.vector.tensor_reduce(lsum[:, :, 0], lexp[:, :, :], AX.X, ALU.add).then_inc(lsum_done, 1)
                    wait(dve, lsum_done, count(b, 1, 1))
                    nc.vector.reciprocal(lrec[:, :, :], lsum[:, :, :]).then_inc(lrec_done, 1)
                    wait(dve, lrec_done, count(b, 1, 1))
                    dst = aff[:, :, :].rearrange("p i (e b) -> p i e b", b=BATCH)
                    dst = dst[:, :, :, b:b + 1] if isinstance(b, int) else dst[:, :, :, bass.ds(b, 1)]
                    nc.vector.tensor_tensor(dst.rearrange("p i e o -> p i (e o)"), lexp[:, :, :],
                                            lrec[:, :, :].broadcast_to([P, NT, EXPERTS]),
                                            ALU.mult).then_inc(aff_done, 1)

            rounds(dve, piece)

        @block.gpsimd
        def _(pool):
            def piece(body, p):
                kind, b = p[0], p[1]
                if kind in ("ln1", "ln2"):
                    wait(pool, ln_var[kind], count(b, 1, 1))
                    wait(pool, ln_done[kind], count(b, NT, 0))
                    nc.gpsimd.tensor_tensor(out=rstd[kind][:, :], in0=var_eps[kind][:, :], in1=minus_half[:, :],
                                            op=ALU.pow).then_inc(ln_rstd[kind], 1)
                elif kind in ("q+", "k+"):
                    job, t = kind[0], p[2]
                    wait_apart(pool, read[job], count(b, 2, t + 1), passed["pool"])
                    nc.gpsimd.tensor_copy(parts[job][:, 1, t, :], rest[:, t, :]).then_inc(part_mid, 1)
                    wait(pool, part_mid, count(b, 4, t + (2 if job == "k" else 0) + 1))
                    nc.gpsimd.tensor_tensor(out=parts[job][:, 2, t, :], in0=rest[:, t, :],
                                            in1=parts[job][:, 1, t, :], op=ALU.subtract).then_inc(rest_split, 1)
                elif kind == "vaug":
                    wait(pool, pv_filled, count(b, GROUPS, 0))
                    wait_apart(pool, read["v"], count(b, 2, 2), passed["pool"])
                    nc.gpsimd.tensor_copy(v_aug[:, :, :, 0:HD],
                                          v_new[:, :, :].rearrange("p i (h d) -> p i h d", h=HEADS))\
                        .then_inc(vaug_done, 1)
                elif kind == "res":
                    wait(pool, res_loaded, count(b, 16, 16))
                    nc.gpsimd.tensor_tensor(out=res_t[:, :, :], in0=res_t[:, :, :],
                                            in1=bias[:, :].unsqueeze(1).broadcast_to([P, NT, D]),
                                            op=ALU.add).then_inc(res_done, 1)
                elif kind == "xs":
                    wait(pool, ln_done["ln2"], count(b, NT, NT))
                    wait_apart(pool, tok_stored, count(b, 16, 0), passed["pool"])
                    nc.gpsimd.tensor_copy(tok[:, :, 0:D], xn2[:, :, :]).then_inc(tok_hi, 1)
                    wait(pool, tok_hi, count(b, 1, 1))
                    nc.gpsimd.tensor_tensor(out=tok[:, :, D:2 * D], in0=xn2[:, :, :], in1=tok[:, :, 0:D],
                                            op=ALU.subtract).then_inc(tok_lo, 1)

            part_mid = sem("part_mid")
            rounds(pool, piece)


def experts(nc, ctx, sb, sem, g):
    ident, identb, aff, tanh_g, passed = g["ident"], g["identb"], g["aff"], g["tanh_g"], g["passed"]
    bank, tok_dram = g["bank"], g["tok_dram"]
    out_rows = g["out"].rearrange("b t d -> (b t) d")
    gate_bank, up_bank, y_bank, tok_bank, w_bank = bank[0:2], bank[2:4], bank[4:6], bank[6], bank[7]

    CHUNK = BATCH // 4
    CHUNKS = BATCH // CHUNK
    IT = INNER // P
    WJOBS = 12
    ROUNDS = SLOTS // 8

    work = sb(ctx, "work", [P, T], F32)
    top = sb(ctx, "top", [P, SLOTS], F32)
    top_at = sb(ctx, "top_at", [P, SLOTS], U32)
    top_atf = sb(ctx, "top_atf", [P, SLOTS], F32)
    batch_base = sb(ctx, "batch_base", [P, EXPERTS * BATCH], F32)
    row_of = sb(ctx, "row_of", [P, EXPERTS * BATCH], U32)
    gating = sb(ctx, "gating", [P, EXPERTS * BATCH], F32)
    row_now = sb(ctx, "row_now", [P, 2, BATCH], U32)
    gate_now = sb(ctx, "gate_now", [P, 2, BATCH], F32)

    w_raw = {"gate": sb(ctx, "gate_raw", [P, IT, D], F32), "up": sb(ctx, "up_raw", [P, IT, D], F32),
             "down": sb(ctx, "down_raw", [P, NH2, INNER], F32)}
    w_in = {n: sb(ctx, f"{n}T", [P, 2, 2, NH2, INNER], BF16) for n in ("gate", "up")}
    w_out = sb(ctx, "downT", [P, 2, 2, IT, D], BF16)
    rows = sb(ctx, "rows", [P, 2, CHUNK, 2 * D], BF16)
    tokT = sb(ctx, "tokT", [P, 2, 2, NH2, T], BF16)
    silu = sb(ctx, "silu", [P, 2, T], F32)
    h32 = sb(ctx, "h32", [P, 2, T], F32)
    h = sb(ctx, "h", [P, 2, 2, IT, T], BF16)
    y = sb(ctx, "y", [P, 2, CHUNK, D], F32)

    names = ("rows_turned", "rows_copied", "top_found", "top_located", "top_taken", "at_float", "top_turned",
             "base_made", "row_made", "gating_made", "row_now_made", "gate_now_made", "w_turned", "w_hi", "w_lo",
             "tok_turned", "tok_read", "gate_filled", "up_filled", "silu_done", "h_done", "h_hi", "h_lo",
             "down_done", "y_read")
    S = {n: sem(n) for n in names}
    raw_loaded = {n: sem(f"{n}_raw_loaded") for n in w_raw}
    gathered = [[sem(f"gathered{i}{j}") for j in range(CHUNK)] for i in range(2)]
    scattered = [[sem(f"scattered{i}{j}") for j in range(CHUNK)] for i in range(2)]
    PARTS = ("gate", "up", "down")

    def schedule(pair):
        order = []
        for par in range(2):
            e = pair * 2 + par
            for c in range(CHUNKS):
                nxt = (e, par, c + 1) if c + 1 < CHUNKS else (e + 1, 1 - par, 0)
                aft = (e, par, c + 2) if c + 2 < CHUNKS else (e + 1, 1 - par, c + 2 - CHUNKS)
                last = (e, par, c - 1) if c else (e - 1, 1 - par, CHUNKS - 1)
                if c == 1:
                    order.append(("columns", e + 1, 1 - par, 0))
                order += [("gather", *aft, s) for s in range(CHUNK)]
                for it in range(IT):
                    order.append(("up", e, par, c, it))
                    if it in (0, 2, 4, 6):
                        order.append(("tok", *nxt, it // 2))
                    if it in (1, 3, 5):
                        order.append(("weights", e + 1, 1 - par, 0, 3 * c + it // 2))
                    if it == 7 and c in (1, 2, 3):
                        order.append(("load", e + 2, par, 0, PARTS[c - 1]))
                order += [("down", *last, s) for s in range(CHUNK)]
        return [p for p in order if not isinstance(p[1], int) or 0 <= p[1] < EXPERTS]

    def run(eng, piece, first, final):
        for p in first:
            piece(p)
        for p in schedule(0):
            piece(p)
        with eng.Fori(1, EXPERTS // 2 - 1) as pair:
            for p in schedule(pair):
                piece(p)
        for p in schedule(EXPERTS // 2 - 1):
            piece(p)
        for p in final:
            piece(p)

    BEFORE = ([("load", 0, 0, 0, n) for n in PARTS] + [("weights", 0, 0, 0, k) for k in range(WJOBS)]
              + [("load", 1, 1, 0, n) for n in PARTS] + [("columns", 0, 0, 0)]
              + [("gather", 0, 0, c, s) for c in range(2) for s in range(CHUNK)]
              + [("tok", 0, 0, 0, s) for s in range(CHUNK)])
    AFTER = [("down", EXPERTS - 1, 1, CHUNKS - 1, s) for s in range(CHUNK)]

    with nc.Block() as block:
        @block.sync
        def _(sp):
            src = {"gate": g["w_gate"], "up": g["w_up"], "down": g["w_down"]}

            def piece(p):
                if p[0] == "load":
                    _, e, _, _, n = p
                    wait(sp, S["w_turned"], (e - 1) * WJOBS + 4 * (PARTS.index(n) + 1))
                    sp.dma_start(w_raw[n][:, :, :], src[n][e].rearrange("(o p) i -> p o i", p=P))\
                        .then_inc(raw_loaded[n], 16)

            run(sp, piece, BEFORE, AFTER)

        @block.gpsimd
        def _(pool):
            nc.gpsimd.iota(batch_base[:, :], pattern=[[0, EXPERTS], [T, BATCH]], base=0, channel_multiplier=0,
                           allow_small_or_imprecise_dtypes=True).then_inc(S["base_made"], 1)

            def piece(p):
                kind, e, par, c = p[:4]
                n = e * CHUNKS + c
                if kind == "gather":
                    s = p[4]
                    if s == 0:
                        wait(pool, S["row_now_made"], e + 1)
                        wait_apart(pool, S["tok_turned"], (n - 1) * CHUNK, passed["pool"])
                    nc.gpsimd.indirect_dma_start(
                        rows[:, c % 2, s, :], None, tok_dram[:, :],
                        bass.IndirectOffsetOnAxis(ap=row_now[:, par, CHUNK * c + s:CHUNK * c + s + 1], axis=0))\
                        .then_inc(gathered[c % 2][s], 16)
                elif kind == "down":
                    s = p[4]
                    wait_apart(pool, S["y_read"], n * CHUNK + s + 1, passed["pool"])
                    nc.gpsimd.indirect_dma_start(
                        out_rows, bass.IndirectOffsetOnAxis(
                            ap=row_now[:, par, CHUNK * c + s:CHUNK * c + s + 1], axis=0),
                        y[:, c % 2, s, :], None, compute_op=ALU.add).then_inc(scattered[c % 2][s], 16)

            run(pool, piece, BEFORE, AFTER)
            for i in range(2):
                for s in range(CHUNK):
                    pool.wait_ge(scattered[i][s], 16 * EXPERTS * CHUNKS // 2)

        @block.tensor
        def _(pe):
            for i in range(NT):
                last = nc.tensor.transpose(gate_bank[0][:, i * P:(i + 1) * P], aff[:, i, :], ident[:, :])
            last.then_inc(S["rows_turned"], 1)

            def piece(p):
                kind, e, par, c = p[:4]
                n = e * CHUNKS + c
                if kind == "weights":
                    k = p[4]
                    part, q = PARTS[k // 4], k % 4
                    wait(pe, raw_loaded[part], (e + 1) * 16)
                    wait(pe, S["w_lo"], e * WJOBS + k)
                    for j in range(4):
                        if part == "down":
                            it, dh = 2 * q + j // 2, j % 2
                            src = w_raw[part][:, dh, it * P:(it + 1) * P]
                        else:
                            dh, it = q // 2, 4 * (q % 2) + j
                            src = w_raw[part][:, it, dh * P:(dh + 1) * P]
                        last = nc.tensor.transpose(w_bank[:, j * P:(j + 1) * P], src, ident[:, :])
                    last.then_inc(S["w_turned"], 1)
                elif kind == "columns" and isinstance(e, int) and e == 0:
                    pe.wait_ge(S["at_float"], 1)
                    pe.wait_ge(S["top_found"], ROUNDS)
                    nc.tensor.transpose(gate_bank[1][:, 0:P], top_atf[:, :], ident[:, :])
                    nc.tensor.transpose(gate_bank[1][:, P:2 * P], top[:, :], ident[:, :]).then_inc(S["top_turned"], 1)
                elif kind == "tok":
                    s = p[4]
                    wait(pe, gathered[c % 2][s], (e * 2 + c // 2 + 1) * 16)
                    wait(pe, S["tok_read"], n * CHUNK + s)
                    to = tok_bank[:, :].bitcast(BF16)
                    for j in range(4):
                        last = nc.tensor.transpose(to[:, j * P:(j + 1) * P], rows[:, c % 2, s, j * P:(j + 1) * P],
                                                   identb[:, :])
                    last.then_inc(S["tok_turned"], 1)
                elif kind == "up":
                    it = p[4]
                    m = n * IT + it
                    if it == 0:
                        wait(pe, S["tok_read"], (n + 1) * CHUNK)
                        wait(pe, S["w_lo"], (e + 1) * WJOBS)
                    for name, banks, freed, filled in (("gate", gate_bank, "silu_done", "gate_filled"),
                                                       ("up", up_bank, "h_done", "up_filled")):
                        wait(pe, S[freed], m - 1)
                        for dh in range(NH2):
                            hi, lo = (w_in[name][:, par, r, dh, it * P:(it + 1) * P] for r in range(2))
                            xh, xl = (tokT[:, c % 2, r, dh, :] for r in range(2))
                            nc.tensor.matmul(banks[it % 2][:, :], hi, xh, start=(dh == 0), stop=False)
                            nc.tensor.matmul(banks[it % 2][:, :], hi, xl, start=False, stop=False)
                            last = nc.tensor.matmul(banks[it % 2][:, :], lo, xh, start=False, stop=(dh == NH2 - 1))
                        last.then_inc(S[filled], 1)
                elif kind == "down":
                    s = p[4]
                    if s == 0:
                        wait(pe, S["h_lo"], (n + 1) * IT)
                    if s % 2 == 0:
                        wait(pe, S["y_read"], (n - 1) * CHUNK + s + 2)
                    to = y_bank[s // 2][:, (s % 2) * D:(s % 2 + 1) * D]
                    for it in range(IT):
                        hh, hl = (h[:, c % 2, r, it, s * P:(s + 1) * P] for r in range(2))
                        wh, wl = (w_out[:, par, r, it, :] for r in range(2))
                        nc.tensor.matmul(to, hh, wh, start=(it == 0), stop=False)
                        nc.tensor.matmul(to, hh, wl, start=False, stop=False)
                        last = nc.tensor.matmul(to, hl, wh, start=False, stop=(it == IT - 1))
                    last.then_inc(S["down_done"], 1)

            run(pe, piece, BEFORE, AFTER)

        def weights_dst(par, r, k):
            part, q = PARTS[k // 4], k % 4
            if part == "down":
                return w_out[:, par, r, 2 * q:2 * q + 2, :].rearrange("p i d -> p (i d)")
            return w_in[part][:, par, r, q // 2, (q % 2) * 512:(q % 2 + 1) * 512]

        @block.scalar
        def _(act):
            def piece(p):
                kind, e, par, c = p[:4]
                n = e * CHUNKS + c
                if kind == "weights":
                    k = p[4]
                    wait(act, S["w_turned"], e * WJOBS + k + 1)
                    if k == 0:
                        wait(act, S["up_filled"], (e - 1) * CHUNKS * IT)
                    if k == 8:
                        wait(act, S["down_done"], (e - 1) * CHUNKS * CHUNK)
                    nc.scalar.activation(weights_dst(par, 0, k), w_bank[:, :], ACT.Copy).then_inc(S["w_hi"], 1)
                elif kind == "up":
                    it = p[4]
                    m = n * IT + it
                    wait(act, S["gate_filled"], m + 1)
                    wait(act, S["h_done"], m - 1)
                    nc.scalar.activation(silu[:, it % 2, :], gate_bank[it % 2][:, :], ACT.Silu)\
                        .then_inc(S["silu_done"], 1)
                    wait(act, S["h_done"], m + 1)
                    if it == 0:
                        wait(act, S["down_done"], (n - 1) * CHUNK)
                    nc.scalar.activation(h[:, c % 2, 0, it, :], h32[:, it % 2, :], ACT.Copy).then_inc(S["h_hi"], 1)
                elif kind == "down":
                    s = p[4]
                    if s % 2 == 0:
                        wait(act, S["down_done"], n * CHUNK + s + 2)
                    wait(act, scattered[c % 2][s], (e * 2 + c // 2) * 16)
                    col = CHUNK * c + s
                    nc.scalar.activation(y[:, c % 2, s, :], y_bank[s // 2][:, (s % 2) * D:(s % 2 + 1) * D],
                                         ACT.Copy, scale=gate_now[:, par, col:col + 1]).then_inc(S["y_read"], 1)

            run(act, piece, BEFORE, AFTER)

        @block.vector
        def _(dve):
            dve.wait_ge(S["rows_turned"], 1)
            nc.vector.tensor_copy(work[:, :], gate_bank[0][:, :]).then_inc(S["rows_copied"], 1)
            dve.wait_ge(S["rows_copied"], 1)
            for r in range(ROUNDS):
                at = slice(8 * r, 8 * r + 8)
                nc.vector.max(top[:, at], work[:, :]).then_inc(S["top_found"], 1)
                dve.wait_ge(S["top_found"], r + 1)
                nc.vector.max_index(top_at[:, at], top[:, at], work[:, :]).then_inc(S["top_located"], 1)
                dve.wait_ge(S["top_located"], r + 1)
                if r < ROUNDS - 1:
                    nc.vector.match_replace(work[:, :], top[:, at], work[:, :], -1.0).then_inc(S["top_taken"], 1)
                    dve.wait_ge(S["top_taken"], r + 1)
            nc.vector.tensor_copy(top_atf[:, :], top_at[:, :]).then_inc(S["at_float"], 1)

            def piece(p):
                kind, e, par, c = p[:4]
                n = e * CHUNKS + c
                if kind == "weights":
                    k = p[4]
                    wait(dve, S["w_hi"], e * WJOBS + k + 1)
                    nc.vector.tensor_tensor(weights_dst(par, 1, k), w_bank[:, :], weights_dst(par, 0, k),
                                            ALU.subtract).then_inc(S["w_lo"], 1)
                elif kind == "columns":
                    if isinstance(e, int) and e == 0:
                        dve.wait_ge(S["top_turned"], 1)
                        dve.wait_ge(S["base_made"], 1)
                        nc.vector.tensor_tensor(row_of[:, :], gate_bank[1][:, 0:P], batch_base[:, :], ALU.add)\
                            .then_inc(S["row_made"], 1)
                        nc.vector.tensor_scalar(gating[:, :], gate_bank[1][:, P:2 * P], tanh_g[:, 1:2], None,
                                                ALU.mult).then_inc(S["gating_made"], 1)
                        dve.wait_ge(S["row_made"], 1)
                        dve.wait_ge(S["gating_made"], 1)
                    for s in range(CHUNK):
                        wait(dve, scattered[1][s], (e - 1) * 2 * 16)
                    cols = slice(e * BATCH, (e + 1) * BATCH) if isinstance(e, int) else bass.ds(e * BATCH, BATCH)
                    nc.vector.tensor_copy(row_now[:, par, :], row_of[:, cols]).then_inc(S["row_now_made"], 1)
                    nc.vector.tensor_copy(gate_now[:, par, :], gating[:, cols]).then_inc(S["gate_now_made"], 1)
                elif kind == "tok":
                    s = p[4]
                    wait(dve, S["tok_turned"], n * CHUNK + s + 1)
                    if s == 0:
                        wait(dve, S["up_filled"], (n - 1) * IT)
                    dst = tokT[:, c % 2, :, :, s * P:(s + 1) * P].rearrange("p r d t -> p (r d) t")
                    nc.vector.tensor_copy(dst, tok_bank[:, :].bitcast(BF16)[:, 0:4 * P].rearrange(
                        "p (j t) -> p j t", j=4)).then_inc(S["tok_read"], 1)
                elif kind == "up":
                    it = p[4]
                    m = n * IT + it
                    wait(dve, S["silu_done"], m + 1)
                    wait(dve, S["up_filled"], m + 1)
                    wait(dve, S["h_lo"], m - 1)
                    nc.vector.tensor_tensor(h32[:, it % 2, :], up_bank[it % 2][:, :], silu[:, it % 2, :], ALU.mult)\
                        .then_inc(S["h_done"], 1)
                    wait(dve, S["h_hi"], m + 1)
                    nc.vector.tensor_tensor(h[:, c % 2, 1, it, :], h32[:, it % 2, :], h[:, c % 2, 0, it, :],
                                            ALU.subtract).then_inc(S["h_lo"], 1)

            run(dve, piece, BEFORE, AFTER)


INPUTS = ["x", "ctx_1024", "g_xattn", "g_ffn", "L0_xattn_Wq", "L0_xattn_Wk", "L0_xattn_Wv", "L0_xattn_Wo",
          "L0_xattn_bo", "L0_ffn_gate_w", "L0_ffn_w_gate", "L0_ffn_w_up", "L0_ffn_w_down"]


def kernel(**inputs):
    import numpy as np
    import concourse.bacc as bacc
    from concourse.bass_utils import run_bass_kernel_spmd

    nc = bacc.Bacc("TRN2", target_bir_lowering=False, num_devices=1)
    arrays, args = {}, []
    for name in INPUTS:
        a = np.ascontiguousarray(inputs[name])
        arrays[f"in_{name}"] = a
        args.append(nc.dram_tensor(f"in_{name}", a.shape, mybir.dt.from_np(a.dtype), kind="ExternalInput").ap())
    args.append(nc.dram_tensor("out_0", (BATCH, T, D), F32, kind="ExternalOutput").ap())
    flamingo(nc, *args)
    r = run_bass_kernel_spmd(nc, [arrays], core_ids=[0])
    return r.results[0]["out_0"]
```

```python
from contextlib import ExitStack

import concourse.bass as bass
from concourse import mybir

ALU = mybir.AluOpType
ACT = mybir.ActivationFunctionType
AX = mybir.AxisListType
F32 = mybir.dt.float32
BF16 = mybir.dt.bfloat16
U32 = mybir.dt.uint32

P = 128
BATCH = 16
T = 512
D = 256
HEADS = 16
HD = D // HEADS
NT = T // P
NH2 = D // P
GROUPS = 4
GH = HEADS // GROUPS
EXPERTS = 8
SLOTS = T // EXPERTS * 2
INNER = 1024
EPS = 1e-5
NEG = -1e30

PRODUCTS = [(c, rw, rs) for c in range(NH2) for rw, rs in ((0, 0), (0, 1), (1, 0))]

STACK = 6 * HD
ROWS = STACK + 2

MAX_UNITS = [(0, 0, 4), (1, 0, 2), (1, 2, 2)] + [(i, h, 1) for i in (2, 3) for h in range(GH)]
NMAX = len(MAX_UNITS)
SC_UNITS = []
for _h in (0, 2):
    SC_UNITS += [(_h, 1, (0,)), (_h, 1, (1, 3)), (_h + 1, 1, (0,)), (_h + 1, 1, (1, 3)), (_h, 2, (2,))]
NSC = len(SC_UNITS)
SC_BANK = [0, 1, 2, 0, 1, 2, 0, 1, 2, 1]
SC_BEFORE = [6 - NSC, 9 - NSC, 8 - NSC, 0, 1, 2, 3, 4, 5, 7]
PWIDTH = [T - P * j for j in range(NT)]
POFF = [0, 512, 1024, 896]
PALL = sum(PWIDTH)


def starts_job(p):
    return p[0] in JOBS_A_BATCH and (len(p) < 4 or p[3] == 0)


def steps(body):
    b = body
    order = []
    extra = {
        0: {0: [("pv", b - 1, 1, 0), ("ln1+", b + 1, 0)], 1: [("yt", b - 1, 0), ("pv", b - 1, 1, 1)],
            2: [("yt+", b - 1, 0), ("yb", b - 2, 1)],
            3: [("pv", b - 1, 1, 2), ("mrow", b - 1, 3), ("yb+", b - 2, 1)],
            4: [("mt+", b - 1, 3), ("mt", b - 1, 3)],
            5: [("pv", b - 1, 1, 3), ("o+", b - 2, 0), ("o", b - 2, 0, 0), ("o", b - 2, 0, 1), ("ln1+", b + 1, 1)],
            6: [("pv+", b - 1, 1)],
            7: [("o", b - 2, 1, 0), ("o", b - 2, 1, 1), ("o+", b - 2, 1), ("tx", b + 1, 0), ("tx+", b + 1, 0)],
            9: [("tx", b + 1, 1), ("tx+", b + 1, 1)], 10: [("yt", b - 1, 1), ("stack", b, 2)]},
        1: {1: [("mt", b, 0)], 2: [("yt+", b - 1, 1)],
            3: [("pv", b - 1, 2, 0), ("mt+", b, 0), ("ln2", b - 2, 0)],
            4: [("q", b + 1, 0, 0), ("q", b + 1, 0, 1), ("q+", b + 1, 0)],
            5: [("pv", b - 1, 2, 1), ("ln2", b - 2, 1)],
            6: [("q", b + 1, 1, 0), ("q", b + 1, 1, 1), ("q+", b + 1, 1)],
            7: [("pv", b - 1, 2, 2), ("tc", b + 1, 0), ("tc+", b + 1, 0)], 8: [("mrow", b, 0), ("tc", b + 1, 1)],
            9: [("pv", b - 1, 2, 3), ("xs", b - 2), ("ln2+", b - 2, 1)],
            10: [("pv+", b - 1, 2), ("ln2+", b - 2, 0), ("pv", b - 1, 3, 0), ("tc+", b + 1, 1)]},
        2: {1: [("stack", b, 3), ("qstore", b + 1), ("mt", b, 1), ("mt+", b, 1), ("pv", b - 1, 3, 1)],
            2: [("yt+", b - 1, 2), ("mrow", b, 1)],
            3: [("yt", b - 1, 2), ("yb", b - 1, 0), ("yb+", b - 1, 0), ("k+", b + 1, 0)],
            4: [("k", b + 1, 0, 0), ("k", b + 1, 0, 1), ("pv", b - 1, 3, 2)],
            5: [("k", b + 1, 1, 0), ("pv", b - 1, 3, 3), ("load", b + 2), ("k+", b + 1, 1), ("k", b + 1, 1, 1)],
            7: [("pv+", b - 1, 3), ("vaug", b)], 8: [("xt+", b - 2, 0), ("res", b - 1), ("xt", b - 2, 0)],
            9: [("xt", b - 2, 1)], 10: [("xt+", b - 2, 1)]},
        3: {0: [("kstore", b + 1)], 1: [("mt", b, 2)],
            2: [("mrow", b, 2), ("mt+", b, 2), ("yt", b - 1, 3), ("yt+", b - 1, 3)], 3: [("ll+", b - 2)],
            4: [("pv", b, 0, 0), ("ll", b - 2), ("v", b + 1, 0, 0), ("v", b + 1, 0, 1), ("v+", b + 1, 0)],
            5: [("ln1", b + 2, 0)], 6: [("stack", b + 1, 0), ("lt", b - 2), ("lt+", b - 2), ("pv", b, 0, 1)],
            8: [("v+", b + 1, 1), ("v", b + 1, 1, 0), ("pv", b, 0, 2), ("v", b + 1, 1, 1)],
            9: [("stack", b + 1, 1)], 10: [("pv+", b, 0), ("pv", b, 0, 3), ("save", b - 2), ("ln1", b + 2, 1)]},
    }
    for g in range(GROUPS):
        sc = (b, g - 2) if g >= 2 else (b - 1, g + 2)
        for k in range(NMAX):
            order.append(("max", b, g, k))
            if k < NSC:
                order.append(("sc", *sc, k))
            order += extra[g].get(k, [])
    return [p for p in order if not isinstance(p[1], int) or 0 <= p[1] < BATCH]


def key(p):
    return (p[0], p[2] if len(p) > 2 else 0)


JOBS_A_BATCH = {"yt": 4, "yb": 2, "o": 2, "tx": 2, "tc": 2, "mt": 4, "q": 2, "k": 2, "xt": 2, "ll": 1, "lt": 1, "v": 2}
JOB_BANK = {job: i % 2 for i, job in enumerate(key(p) for p in steps(BATCH // 2) if starts_job(p))}


def count(b, per, k):
    return b * per + k


def wait(eng, s, value):
    if not isinstance(value, int) or value > 0:
        eng.wait_ge(s, value)


def wait_apart(eng, s, value, passed):
    wait(eng, s, value)
    if not isinstance(value, int):
        eng.sem_inc(passed, 1)


def flamingo(nc, x, ctx_kv, g_xattn, g_ffn, wq, wk, wv, wo, bo, gate_w, w_gate, w_up, w_down, out):
    with ExitStack() as stack:
        def sem(name):
            return stack.enter_context(nc.semaphore(name))

        def sb(ctx, name, shape, dt):
            return ctx.enter_context(nc.sbuf_tensor(name, shape, dt))

        bank = [stack.enter_context(nc.psum_tensor(f"bank{i}", [P, 512], F32)) for i in range(8)]
        max_bank, sc_bank, pv_bank, job_bank = bank[0:2], bank[2:5], bank[5], bank[6:8]

        q_dram = nc.dram_tensor("q_parts", [BATCH, GROUPS, 3, HD * GH, T], BF16, kind="Internal").ap()
        k_dram = nc.dram_tensor("k_parts", [BATCH, GROUPS, 3, HD * GH, T], BF16, kind="Internal").ap()
        m_dram = nc.dram_tensor("m_parts", [BATCH, GROUPS, 2, GH * NT, P], BF16, kind="Internal").ap()
        tok_dram = nc.dram_tensor("tokens", [BATCH * T, 2 * D], BF16, kind="Internal").ap()

        ident = sb(stack, "ident", [P, P], F32)
        identb = sb(stack, "identb", [P, P], BF16)
        aff = sb(stack, "aff", [P, NT, EXPERTS * BATCH], F32)
        tanh_g = sb(stack, "tanh_g", [P, 2], F32)
        passed = {n: sem(f"passed_{n}") for n in ("dve", "pool", "sp")}

        with ExitStack() as ctx:
            attention(nc, ctx, stack, sb, sem, locals())
        with ExitStack() as ctx:
            experts(nc, ctx, sb, sem, locals())


def attention(nc, ctx, stack, sb, sem, g):
    x, ctx_kv, out = g["x"], g["ctx_kv"], g["out"]
    ident, identb, aff, tanh_g, passed = g["ident"], g["identb"], g["aff"], g["tanh_g"], g["passed"]
    max_bank, sc_bank, pv_bank, job_bank = g["max_bank"], g["sc_bank"], g["pv_bank"], g["job_bank"]
    q_dram, k_dram, m_dram, tok_dram = g["q_dram"], g["k_dram"], g["m_dram"], g["tok_dram"]

    mask_qk = sb(ctx, "mask_qk", [P, P], BF16)
    mask_kq = sb(ctx, "mask_kq", [P, P], BF16)
    wT = {n: sb(ctx, f"{n}T", [P, 2, NH2, D], BF16) for n in ("wq", "wk", "wv", "wo")}
    gwT = sb(ctx, "gwT", [P, NH2, 32], F32)
    llT = sb(ctx, "llT", [P, P], F32)
    bias = sb(ctx, "bias", [P, D], F32)
    minus_half = sb(ctx, "minus_half", [P, NT], F32)

    x_t = sb(ctx, "x_t", [P, NT, D], F32)
    ctx_t = sb(ctx, "ctx_t", [P, NT, D], F32)
    res_t = sb(ctx, "res_t", [P, NT, D], F32)
    xn = sb(ctx, "xn", [P, NT, D], F32)
    xT = sb(ctx, "xT", [P, 2, NH2, T], BF16)
    cT = sb(ctx, "cT", [P, 2, NH2, T], BF16)
    parts = {"q": sb(ctx, "q_sb", [P, 3, NH2, T], BF16), "k": sb(ctx, "k_sb", [P, 3, NH2, T], BF16)}
    rest = sb(ctx, "rest", [P, 2, T], F32)
    qs = sb(ctx, "qs", [ROWS, GROUPS, GH, T], BF16)
    ks = sb(ctx, "ks", [ROWS, GROUPS, GH, T], BF16)
    prob = sb(ctx, "prob", [P, 2, GH, PALL], F32)
    v_new = sb(ctx, "v_new", [P, NT, D], F32)
    v_aug = sb(ctx, "v_aug", [P, NT, HEADS, 32], F32)
    mx = sb(ctx, "mx", [P, 2, GH, NT], F32)
    m_parts = sb(ctx, "m_sb", [GH * NT, 2, P], BF16)
    yT = sb(ctx, "yT", [P, T], F32)
    rden = sb(ctx, "rden", [P, NT, GH, 1], F32)
    yq = sb(ctx, "yq", [P, NT, D], F32)
    ynT = sb(ctx, "ynT", [P, 2, NH2, T], BF16)
    x1 = sb(ctx, "x1", [P, NT, D], F32)
    xn2 = sb(ctx, "xn2", [P, NT, D], F32)
    tok = sb(ctx, "tok", [P, NT, 2 * D], BF16)
    xn2T = sb(ctx, "xn2T", [P, NH2, T], F32)
    stats = {n: sb(ctx, f"{n}_stats", [P, NT, 6], F32) for n in ("ln1", "ln2")}
    mean_var = {n: sb(ctx, f"{n}_mv", [P, NT, 2], F32) for n in ("ln1", "ln2")}
    var_eps = {n: sb(ctx, f"{n}_ve", [P, NT], F32) for n in ("ln1", "ln2")}
    rstd = {n: sb(ctx, f"{n}_rstd", [P, NT], F32) for n in ("ln1", "ln2")}
    lmax = sb(ctx, "lmax", [P, NT, 1], F32)
    logit = sb(ctx, "logit", [P, NT, EXPERTS], F32)
    lexp = sb(ctx, "lexp", [P, NT, EXPERTS], F32)
    lsum = sb(ctx, "lsum", [P, NT, 1], F32)
    lrec = sb(ctx, "lrec", [P, NT, 1], F32)

    w_raw = {n: sb(ctx, f"{n}_raw", [P, NH2, D], F32) for n in ("wq", "wk", "wv", "wo")}
    gw_raw = sb(ctx, "gw_raw", [EXPERTS, D], F32)
    gates = sb(ctx, "gates", [P, 2], F32)
    bo_rep = sb(ctx, "bo_rep", [P, D], F32)
    w_loaded = {n: sem(f"{n}_loaded") for n in ("wq", "wk", "wv", "wo", "gate_w")}
    gates_loaded, consts, cast, turned, hi_taken, evac, tanh_done, bias_done = (
        sem(n) for n in ("gates_loaded", "consts", "cast", "turned", "hi_taken", "evac", "tanh_done", "bias_done"))
    order = [(n, o) for n in ("wq", "wk", "wv", "wo") for o in range(NH2)]
    CONSTS = 9

    def turned_weights(name, o, i, r, src_bank):
        dst, src = wT[name][:, r, i, o * P:(o + 1) * P], src_bank[:, i * P:(i + 1) * P]
        if name in ("wq", "wk"):
            dst = dst.rearrange("p (g d h) -> p g h d", g=2, h=GH)
            src = src.rearrange("p (g h d) -> p g h d", g=2, h=GH)
        return dst, src

    x_loaded, ctx_loaded, res_loaded = sem("x_loaded"), sem("ctx_loaded"), sem("res_loaded")
    stack_loaded = [sem(f"stack_loaded{i}") for i in range(GROUPS)]
    mrow_loaded = [sem(f"mrow_loaded{i}") for i in range(GROUPS)]
    stored = {n: sem(f"{n}_stored") for n in ("q", "k")}
    mrow_stored, x1_stored, tok_stored = sem("mrow_stored"), sem("x1_stored"), sem("tok_stored")
    filled = {n: sem(f"{n}_filled") for n in JOBS_A_BATCH}
    read = {n: sem(f"{n}_read") for n in JOBS_A_BATCH}
    hi_done = {n: sem(f"{n}_hi_done") for n in ("q", "k", "mt", "tx", "tc", "yb")}
    rest_split = sem("rest_split")
    max_filled, max_read = sem("max_filled"), sem("max_read")
    sc_filled, exp_done = sem("sc_filled"), sem("exp_done")
    pv_filled, pv_read = sem("pv_filled"), sem("pv_read")
    rden_done, vaug_done, res_done = sem("rden_done"), sem("vaug_done"), sem("res_done")
    ln_stats = {n: sem(f"{n}_stats_done") for n in ("ln1", "ln2")}
    ln_aggr = {n: sem(f"{n}_aggr_done") for n in ("ln1", "ln2")}
    ln_var = {n: sem(f"{n}_var_done") for n in ("ln1", "ln2")}
    ln_rstd = {n: sem(f"{n}_rstd_done") for n in ("ln1", "ln2")}
    ln_done = {n: sem(f"{n}_done") for n in ("ln1", "ln2")}
    tok_hi, tok_lo = sem("tok_hi"), sem("tok_lo")
    lmax_done, lexp_done, lsum_done, lrec_done, aff_done = (
        sem(n) for n in ("lmax_done", "lexp_done", "lsum_done", "lrec_done", "aff_done"))

    def rounds(eng, body):
        for b in (-1, 0, 1, 2):
            for p in steps(b):
                body(b, p)
        with eng.Fori(3, BATCH - 2) as b:
            for p in steps(b):
                body(b, p)
        for b in range(BATCH - 2, BATCH + 2):
            for p in steps(b):
                body(b, p)

    def free_bank(pe, b, p):
        mine = JOB_BANK[key(p)]
        jobs = [q for q in steps(b) if starts_job(q) and JOB_BANK[key(q)] == mine]
        at = [key(q) for q in jobs].index(key(p))
        if at:
            q = jobs[at - 1]
        else:
            q = [q for q in steps(b - 1) if starts_job(q) and JOB_BANK[key(q)] == mine]
            if not q:
                return
            q = q[-1]
        wait(pe, read[q[0]], count(q[1], JOBS_A_BATCH[q[0]], key(q)[1] + 1))

    with nc.Block() as block:
        @block.sync
        def _(sp):
            def hold(s, value):
                wait_apart(sp, s, value, passed["sp"])

            def load(b):
                hold(ln_done["ln1"], count(b, NT, 0))
                sp.dma_start(x_t[:, :, :], x[b].rearrange("(i p) d -> p i d", p=P)).then_inc(x_loaded, 16)
                hold(filled["tc"], count(b, NH2, 0))
                sp.dma_start(ctx_t[:, :, :], ctx_kv[b][0:T, :].rearrange("(i p) d -> p i d", p=P)).then_inc(ctx_loaded, 16)

            def piece(body, p):
                kind, b = p[0], p[1]
                if kind == "load":
                    load(b)
                elif kind == "res":
                    hold(read["o"], count(b, 2, 0))
                    sp.dma_start(res_t[:, :, :], x[b].rearrange("(i p) d -> p i d", p=P)).then_inc(res_loaded, 16)
                elif kind in ("qstore", "kstore"):
                    n = kind[0]
                    hold(rest_split, count(b, 4, 2 if n == "q" else 4))
                    dram = (q_dram if n == "q" else k_dram)[b]
                    for r in range(3):
                        for t in range(NH2):
                            sp.dma_start(dram[2 * t:2 * t + 2, r, :, :], parts[n][:, r, t, :]).then_inc(stored[n], 16)
                elif kind == "stack":
                    gr = p[2]
                    hold(stored["q"], count(b, 96, 96))
                    hold(stored["k"], count(b, 96, 96))
                    hold(sc_filled, count(b, GROUPS * NSC, (gr + 1 - GROUPS) * NSC))
                    at = 0
                    for r in (3, 2, 1):
                        src = q_dram[b][gr][0:r].rearrange("r (d h) t -> (r d) (h t)", h=GH)
                        sp.dma_start(qs[at:at + r * HD, gr, :, :].rearrange("p h t -> p (h t)"), src)\
                            .then_inc(stack_loaded[gr], 16)
                        src = k_dram[b][gr][3 - r:4 - r].rearrange("r (d h) t -> r d (h t)", h=GH)
                        src = src.broadcast_to([r, HD, GH * T])
                        sp.dma_start(ks[at:at + r * HD, gr, :, :].rearrange("p h t -> p (h t)"), src)\
                            .then_inc(stack_loaded[gr], 16)
                        at += r * HD
                elif kind == "mrow":
                    gr = p[2]
                    n = count(b, GROUPS, gr)
                    hold(read["mt"], n + 1)
                    sp.dma_start(m_dram[b][gr].rearrange("r a q -> a r q"), m_parts[:, :, :]).then_inc(mrow_stored, 16)
                    hold(mrow_stored, n * 16 + 16)
                    hold(sc_filled, count(b, GROUPS * NSC, (gr + 1 - GROUPS) * NSC))
                    sp.dma_start(qs[STACK:ROWS, gr, :, :], m_dram[b][gr].rearrange("r (h i) q -> r h (i q)", h=GH))\
                        .then_inc(mrow_loaded[gr], 16)
                elif kind == "save":
                    hold(ln_stats["ln2"], count(b, NT, NT))
                    sp.dma_start(out[b].rearrange("(i p) d -> p i d", p=P), x1[:, :, :]).then_inc(x1_stored, 16)
                    hold(tok_lo, count(b, 1, 1))
                    if isinstance(b, int):
                        dst = tok_dram[b * T:(b + 1) * T, :]
                    else:
                        dst = tok_dram[bass.ts(b, T), :]
                    sp.dma_start(dst.rearrange("(i p) d -> p i d", p=P), tok[:, :, :]).then_inc(tok_stored, 16)

            def load_weights(n):
                sp.dma_start(w_raw[n][:, :, :], g[n].rearrange("(o p) i -> p o i", p=P)).then_inc(w_loaded[n], 16)

            load_weights("wq")
            load(0)
            for n in ("wk", "wv", "wo"):
                load_weights(n)
            sp.dma_start(gw_raw[:, :], g["gate_w"]).then_inc(w_loaded["gate_w"], 16)
            sp.dma_start(bo_rep[:, :], g["bo"].partition_broadcast(P)).then_inc(gates_loaded, 16)
            sp.dma_start(gates[:, 0:1], g["g_xattn"].partition_broadcast(P)).then_inc(gates_loaded, 16)
            sp.dma_start(gates[:, 1:2], g["g_ffn"].partition_broadcast(P)).then_inc(gates_loaded, 16)
            rounds(sp, piece)
            sp.wait_ge(x1_stored, 16 * BATCH)
            sp.wait_ge(tok_stored, 16 * BATCH)

        @block.tensor
        def _(pe):
            pe.wait_ge(consts, CONSTS)
            for n, (name, o) in enumerate(order):
                pe.wait_ge(w_loaded[name], 16)
                if n >= 2:
                    pe.wait_ge(evac, n - 1)
                for i in range(NH2):
                    last = nc.tensor.transpose(job_bank[n % 2][:, i * P:(i + 1) * P],
                                               w_raw[name][:, o, i * P:(i + 1) * P], ident[:, :])
                last.then_inc(turned, 1)
            n = len(order)
            pe.wait_ge(w_loaded["gate_w"], 16)
            pe.wait_ge(evac, n - 1)
            for i in range(NH2):
                last = nc.tensor.transpose(job_bank[n % 2][:, i * EXPERTS:(i + 1) * EXPERTS],
                                           gw_raw[:, i * P:(i + 1) * P], ident[0:EXPERTS, 0:EXPERTS])
            last.then_inc(turned, 1)
            pe.wait_ge(evac, n + 1)
            pe.wait_ge(cast, 2)

            def piece(body, p):
                kind, b = p[0], p[1]
                if starts_job(p):
                    free_bank(pe, body, p)
                if key(p) in JOB_BANK:
                    to = job_bank[JOB_BANK[key(p)]]
                if kind == "max":
                    gr, k = p[2], p[3]
                    i, h0, nh = MAX_UNITS[k]
                    n = count(b, GROUPS * NMAX, gr * NMAX + k)
                    if k == 0:
                        wait(pe, stack_loaded[gr], count(b, 96, 96))
                    wait(pe, max_read, n - 1)
                    w = P * (i + 1)
                    dst = max_bank[(gr * NMAX + k) % 2]
                    for h in range(nh):
                        nc.tensor.matmul(dst[:, h * w:(h + 1) * w], qs[0:STACK, gr, h0 + h, i * P:(i + 1) * P],
                                         ks[0:STACK, gr, h0 + h, 0:w], start=True, stop=False)
                        last = nc.tensor.matmul(dst[:, h * w + w - P:(h + 1) * w], identb[:, :], mask_qk[:, :],
                                                start=False, stop=True)
                    last.then_inc(max_filled, 1)
                elif kind == "sc":
                    gr, k = p[2], p[3]
                    h0, nh, tiles = SC_UNITS[k]
                    if k == 0:
                        wait(pe, mrow_loaded[gr], count(b, 16, 16))
                    wait(pe, exp_done, count(b, GROUPS * NSC, gr * NSC + SC_BEFORE[k] + 1))
                    at = 0
                    for h in range(nh):
                        for j in tiles:
                            dst = sc_bank[SC_BANK[k]]
                            nc.tensor.matmul(dst[:, at:at + PWIDTH[j]], ks[:, gr, h0 + h, j * P:(j + 1) * P],
                                             qs[:, gr, h0 + h, j * P:T], start=True, stop=False)
                            last = nc.tensor.matmul(dst[:, at:at + P], identb[:, :], mask_kq[:, :],
                                                    start=False, stop=True)
                            at += PWIDTH[j]
                    last.then_inc(sc_filled, 1)
                elif kind == "pv":
                    gr, j = p[2], p[3]
                    n = count(b, GROUPS, gr)
                    if j == 0:
                        wait(pe, exp_done, (n + 1) * NSC)
                        wait(pe, vaug_done, count(b, 1, 1))
                        wait(pe, pv_read, n)
                    for h in range(GH):
                        last = nc.tensor.matmul(pv_bank[32 * h:32 * h + 32, j * P:T], v_aug[:, j, gr * GH + h, :],
                                                prob[:, gr % 2, h, POFF[j]:POFF[j] + PWIDTH[j]],
                                                start=(j == 0), stop=(j == NT - 1))
                    if j == NT - 1:
                        last.then_inc(pv_filled, 1)
                elif kind == "mt":
                    gr = p[2]
                    wait(pe, max_read, count(b, GROUPS * NMAX, (gr + 1) * NMAX))
                    nc.tensor.transpose(to[0:GH * NT, 0:P], mx[:, gr % 2, :, :].rearrange("p h i -> p (h i)"),
                                        ident[:, :]).then_inc(filled[kind], 1)
                elif kind == "yt":
                    wait(pe, pv_read, count(b, GROUPS, p[2] + 1))
                    for i in range(NT):
                        last = nc.tensor.transpose(to[:, i * P:(i + 1) * P], yT[:, i * P:(i + 1) * P], ident[:, :])
                    last.then_inc(filled[kind], 1)
                elif kind in ("yb", "tx", "tc", "xt"):
                    half = p[2]
                    src = {"yb": yq, "tx": xn, "tc": ctx_t, "xt": xn2}[kind]
                    if kind == "yb":
                        wait(pe, read["yt"], count(b, GROUPS, 2 * half + 2))
                    elif kind == "tx":
                        wait(pe, ln_done["ln1"], count(b, NT, NT))
                    elif kind == "tc":
                        wait(pe, ctx_loaded, count(b, 16, 16))
                    else:
                        wait(pe, ln_done["ln2"], count(b, NT, NT))
                    for i in range(NT):
                        last = nc.tensor.transpose(to[:, i * P:(i + 1) * P], src[:, i, half * P:(half + 1) * P],
                                                   ident[:, :])
                    last.then_inc(filled[kind], 1)
                elif kind in ("q", "k"):
                    t = p[2]
                    src, made = (xT, "tx") if kind == "q" else (cT, "tc")
                    if p[3] == 0:
                        wait(pe, read[made], count(b, 2, 2))
                    for n in range(3 * p[3], 3 * p[3] + 3):
                        c, rw, rs = PRODUCTS[n]
                        last = nc.tensor.matmul(to[:, :], wT["w" + kind][:, rw, c, t * P:(t + 1) * P],
                                                src[:, rs, c, :], start=(n == 0), stop=(n == len(PRODUCTS) - 1))
                    if p[3] == 1:
                        last.then_inc(filled[kind], 1)
                elif kind in ("v", "o"):
                    src, made = (cT, "tc") if kind == "v" else (ynT, "yb")
                    if p[3] == 0:
                        wait(pe, read[made], count(b, 2, 2))
                    i2, i = p[3], 2 * p[2] + p[3]
                    for n, (c, rw, rs) in enumerate(PRODUCTS):
                        last = nc.tensor.matmul(to[:, i2 * D:(i2 + 1) * D], src[:, rs, c, i * P:(i + 1) * P],
                                                wT["w" + kind][:, rw, c, :], start=(n == 0),
                                                stop=(n == len(PRODUCTS) - 1))
                    if p[3] == 1:
                        last.then_inc(filled[kind], 1)
                elif kind == "ll":
                    wait(pe, read["xt"], count(b, 2, 2))
                    for c in range(NH2):
                        for i in range(NT):
                            last = nc.tensor.matmul(to[32 * i:32 * i + 32, 0:P], gwT[:, c, :],
                                                    xn2T[:, c, i * P:(i + 1) * P],
                                                    start=(c == 0), stop=(c == NH2 - 1))
                    last.then_inc(filled[kind], 1)
                elif kind == "lt":
                    wait(pe, read["ll"], count(b, 1, 1))
                    nc.tensor.transpose(to[:, 0:P], llT[:, :], ident[:, :]).then_inc(filled[kind], 1)

            rounds(pe, piece)

        @block.scalar
        def _(act):
            act.wait_ge(gates_loaded, 48)
            nc.scalar.activation(tanh_g[:, :], gates[:, :], ACT.Tanh).then_inc(tanh_done, 1)
            for n, (name, o) in enumerate(order):
                act.wait_ge(turned, n + 1)
                for i in range(NH2):
                    dst, src = turned_weights(name, o, i, 0, job_bank[n % 2])
                    last = nc.scalar.activation(dst, src, ACT.Copy)
                last.then_inc(hi_taken, 1)
            n = len(order)
            act.wait_ge(turned, n + 1)
            act.wait_ge(evac, n)
            nc.scalar.activation(gwT[:, :, 0:EXPERTS], job_bank[n % 2][:, 0:NH2 * EXPERTS].rearrange(
                "p (i c) -> p i c", i=NH2), ACT.Copy).then_inc(evac, 1)

            def piece(body, p):
                kind, b = p[0], p[1]
                job = kind[:-1] if kind.endswith("+") else None
                if job and (job, key(p)[1]) in JOB_BANK:
                    src = job_bank[JOB_BANK[(job, key(p)[1])]]
                if kind == "sc":
                    gr, k = p[2], p[3]
                    h0, nh, tiles = SC_UNITS[k]
                    n = count(b, GROUPS, gr)
                    if k == 0:
                        wait(act, pv_filled, n - 1)
                    wait(act, sc_filled, n * NSC + k + 1)
                    w = sum(PWIDTH[j] for j in tiles)
                    nc.scalar.activation(prob[:, gr % 2, h0:h0 + nh, POFF[tiles[0]]:POFF[tiles[0]] + w],
                                         sc_bank[SC_BANK[k]][:, 0:nh * w].rearrange("p (h w) -> p h w", h=nh),
                                         ACT.Exp, scale=float(HD) ** -0.5).then_inc(exp_done, 1)
                elif kind == "pv+":
                    n = count(b, GROUPS, p[2])
                    wait(act, pv_filled, n + 1)
                    wait(act, filled["yt"], n)
                    nc.scalar.activation(yT[:, :], pv_bank[:, :], ACT.Copy).then_inc(pv_read, 1)
                elif kind == "mt+":
                    n = count(b, GROUPS, p[2])
                    wait(act, filled["mt"], n + 1)
                    wait(act, mrow_stored, n * 16)
                    nc.scalar.activation(m_parts[:, 0, :], src[0:GH * NT, 0:P], ACT.Copy, scale=-1.0)\
                        .then_inc(hi_done["mt"], 1)
                elif kind in ("tx+", "tc+", "yb+", "xt+"):
                    half = p[2]
                    dst, user, per = {"tx": (xT, "q", 2), "tc": (cT, "v", 2), "yb": (ynT, "o", 2),
                                      "xt": (xn2T, "ll", 1)}[job]
                    wait(act, filled[job], count(b, 2, half + 1))
                    wait(act, filled[user], count(b, per, 0))
                    if job == "xt":
                        nc.scalar.activation(dst[:, half, :], src[:, :], ACT.Copy).then_inc(read[job], 1)
                    else:
                        nc.scalar.activation(dst[:, 0, half, :], src[:, :], ACT.Copy).then_inc(hi_done[job], 1)
                elif kind in ("q+", "k+"):
                    t = p[2]
                    wait(act, filled[job], count(b, 2, t + 1))
                    wait(act, stored[job], count(b, 96, 0))
                    nc.scalar.activation(parts[job][:, 0, t, :], src[:, :], ACT.Copy).then_inc(hi_done[job], 1)
                elif kind == "v+":
                    wait(act, filled["v"], count(b, 2, p[2] + 1))
                    wait(act, vaug_done, count(b, 1, 0))
                    nc.scalar.activation(v_new[:, 2 * p[2]:2 * p[2] + 2, :],
                                         src[:, :].rearrange("p (i d) -> p i d", i=2), ACT.Copy).then_inc(read["v"], 1)
                elif kind == "ll+":
                    wait(act, filled["ll"], count(b, 1, 1))
                    wait(act, filled["lt"], count(b, 1, 0))
                    nc.scalar.activation(llT[:, :], src[:, 0:P], ACT.Copy).then_inc(read["ll"], 1)
                elif kind == "lt+":
                    wait(act, read["lt"], count(b, 1, 1))
                    wait(act, aff_done, count(b, 1, 0))
                    nc.scalar.activation(lexp[:, :, :], logit[:, :, :], ACT.Exp).then_inc(lexp_done, 1)

            rounds(act, piece)

        @block.vector
        def _(dve):
            def norm_stats(n, src, b, half):
                for i in (2 * half, 2 * half + 1):
                    nc.vector.bn_stats(stats[n][:, i, :], src[:, i, :]).then_inc(ln_stats[n], 1)
                if half == 0:
                    return
                wait_apart(dve, ln_stats[n], count(b, NT, NT), passed["dve"])
                for i in range(NT):
                    nc.vector.bn_aggr(mean_var[n][:, i, :], stats[n][:, i, :]).then_inc(ln_aggr[n], 1)
                wait(dve, ln_aggr[n], count(b, NT, NT))
                wait(dve, ln_rstd[n], count(b, 1, 0))
                nc.vector.tensor_scalar_add(var_eps[n][:, :], mean_var[n][:, :, 1], EPS).then_inc(ln_var[n], 1)

            def norm_apply(n, dst, src, b, half):
                wait(dve, ln_rstd[n], count(b, 1, 1))
                for i in (2 * half, 2 * half + 1):
                    nc.vector.tensor_scalar(dst[:, i, :], src[:, i, :], mean_var[n][:, i, 0:1],
                                            rstd[n][:, i:i + 1], ALU.subtract, ALU.mult).then_inc(ln_done[n], 1)

            def piece(body, p):
                kind, b = p[0], p[1]
                job = kind[:-1] if kind.endswith("+") else None
                if job and (job, key(p)[1]) in JOB_BANK:
                    src = job_bank[JOB_BANK[(job, key(p)[1])]]
                if kind == "max":
                    gr, k = p[2], p[3]
                    i, h0, nh = MAX_UNITS[k]
                    w = P * (i + 1)
                    if k == 0:
                        wait(dve, filled["mt"], count(b, GROUPS, gr - 1))
                    wait(dve, max_filled, count(b, GROUPS * NMAX, gr * NMAX + k + 1))
                    nc.vector.tensor_reduce(mx[:, gr % 2, h0:h0 + nh, i], max_bank[(gr * NMAX + k) % 2][
                        :, 0:nh * w].rearrange("p (h w) -> p h w", h=nh), AX.X, ALU.max).then_inc(max_read, 1)
                elif kind == "mt+":
                    wait(dve, hi_done["mt"], count(b, GROUPS, p[2] + 1))
                    nc.vector.scalar_tensor_tensor(m_parts[:, 1, :], src[0:GH * NT, 0:P], -1.0, m_parts[:, 0, :],
                                                   ALU.mult, ALU.subtract).then_inc(read["mt"], 1)
                elif kind in ("tx+", "tc+", "yb+"):
                    half = p[2]
                    dst = {"tx": xT, "tc": cT, "yb": ynT}[job]
                    wait(dve, hi_done[job], count(b, 2, half + 1))
                    nc.vector.tensor_tensor(dst[:, 1, half, :], src[:, :], dst[:, 0, half, :], ALU.subtract)\
                        .then_inc(read[job], 1)
                elif kind in ("q+", "k+"):
                    t = p[2]
                    n = count(b, 4, t + (2 if job == "k" else 0))
                    wait(dve, hi_done[job], count(b, 2, t + 1))
                    wait(dve, rest_split, n - 1)
                    nc.vector.tensor_tensor(rest[:, t, :], src[:, :], parts[job][:, 0, t, :], ALU.subtract)\
                        .then_inc(read[job], 1)
                elif kind == "yt+":
                    gr = p[2]
                    n = count(b, GROUPS, gr + 1)
                    wait(dve, filled["yt"], n)
                    view = src[:, :].rearrange("p (i h c) -> p i h c", i=NT, h=GH)
                    nc.vector.reciprocal(rden[:, :, :, :], view[:, :, :, HD:HD + 1]).then_inc(rden_done, 1)
                    wait(dve, rden_done, n)
                    wait(dve, filled["yb"], count(b, 2, gr // 2 - 1))
                    nc.vector.tensor_tensor(
                        yq[:, :, gr * GH * HD:(gr + 1) * GH * HD].rearrange("p i (h d) -> p i h d", h=GH),
                        view[:, :, :, 0:HD], rden[:, :, :, :].broadcast_to([P, NT, GH, HD]), ALU.mult)\
                        .then_inc(read["yt"], 1)
                elif kind == "o+":
                    t = p[2]
                    wait(dve, filled["o"], count(b, 2, t + 1))
                    wait(dve, res_done, count(b, 1, 1))
                    if t == 0:
                        wait(dve, x1_stored, count(b, 16, 0))
                        wait(dve, ln_done["ln2"], count(b, NT, 0))
                    nc.vector.scalar_tensor_tensor(
                        x1[:, 2 * t:2 * t + 2, :], src[:, :].rearrange("p (i d) -> p i d", i=2), tanh_g[:, 0:1],
                        res_t[:, 2 * t:2 * t + 2, :], ALU.mult, ALU.add).then_inc(read["o"], 1)
                elif kind == "ln1":
                    wait(dve, x_loaded, count(b, 16, 16))
                    norm_stats("ln1", x_t, b, p[2])
                elif kind == "ln1+":
                    wait(dve, filled["tx"], count(b, 2, 0))
                    norm_apply("ln1", xn, x_t, b, p[2])
                elif kind == "ln2":
                    wait(dve, read["o"], count(b, 2, 2))
                    norm_stats("ln2", x1, b, p[2])
                elif kind == "ln2+":
                    wait(dve, filled["xt"], count(b, 2, 0))
                    wait(dve, tok_lo, count(b, 1, 0))
                    norm_apply("ln2", xn2, x1, b, p[2])
                elif kind == "vaug":
                    wait(dve, pv_filled, count(b, GROUPS, 0))
                    wait(dve, read["v"], count(b, 2, 2))
                    nc.vector.tensor_copy(v_aug[:, :, :, 0:HD],
                                          v_new[:, :, :].rearrange("p i (h d) -> p i h d", h=HEADS))\
                        .then_inc(vaug_done, 1)
                elif kind == "lt+":
                    wait(dve, filled["lt"], count(b, 1, 1))
                    view = src[:, 0:P].rearrange("p (i e) -> p i e", i=NT)[:, :, 0:EXPERTS]
                    nc.vector.tensor_reduce(lmax[:, :, 0], view, AX.X, ALU.max).then_inc(lmax_done, 1)
                    wait(dve, lmax_done, count(b, 1, 1))
                    wait(dve, lexp_done, count(b, 1, 0))
                    nc.vector.tensor_tensor(logit[:, :, :], view, lmax[:, :, :].broadcast_to([P, NT, EXPERTS]),
                                            ALU.subtract).then_inc(read["lt"], 1)
                    wait(dve, lexp_done, count(b, 1, 1))
                    nc.vector.tensor_reduce(lsum[:, :, 0], lexp[:, :, :], AX.X, ALU.add).then_inc(lsum_done, 1)
                    wait(dve, lsum_done, count(b, 1, 1))
                    nc.vector.reciprocal(lrec[:, :, :], lsum[:, :, :]).then_inc(lrec_done, 1)
                    wait(dve, lrec_done, count(b, 1, 1))
                    dst = aff[:, :, :].rearrange("p i (e b) -> p i e b", b=BATCH)
                    dst = dst[:, :, :, b:b + 1] if isinstance(b, int) else dst[:, :, :, bass.ds(b, 1)]
                    nc.vector.tensor_tensor(dst.rearrange("p i e o -> p i (e o)"), lexp[:, :, :],
                                            lrec[:, :, :].broadcast_to([P, NT, EXPERTS]),
                                            ALU.mult).then_inc(aff_done, 1)

            nc.vector.memset(ks[STACK:ROWS, :, :, :], 1.0).then_inc(cast, 1)
            dve.wait_ge(consts, CONSTS)
            nc.vector.tensor_copy(identb[:, :], ident[:, :]).then_inc(cast, 1)
            piece(-1, ("ln1", 0, 0))
            piece(-1, ("ln1", 0, 1))
            for n, (name, o) in enumerate(order):
                dve.wait_ge(hi_taken, n + 1)
                for i in range(NH2):
                    dst, src = turned_weights(name, o, i, 1, job_bank[n % 2])
                    hi, _ = turned_weights(name, o, i, 0, job_bank[n % 2])
                    last = nc.vector.tensor_tensor(dst, src, hi, ALU.subtract)
                last.then_inc(evac, 1)
            dve.wait_ge(gates_loaded, 48)
            dve.wait_ge(tanh_done, 1)
            nc.vector.tensor_scalar(bias[:, :], bo_rep[:, :], tanh_g[:, 0:1], None, ALU.mult).then_inc(bias_done, 1)
            rounds(dve, piece)

        @block.gpsimd
        def _(pool):
            def piece(body, p):
                kind, b = p[0], p[1]
                if kind in ("ln1", "ln2") and p[2] == 1:
                    wait(pool, ln_var[kind], count(b, 1, 1))
                    wait(pool, ln_done[kind], count(b, NT, 0))
                    nc.gpsimd.tensor_tensor(out=rstd[kind][:, :], in0=var_eps[kind][:, :], in1=minus_half[:, :],
                                            op=ALU.pow).then_inc(ln_rstd[kind], 1)
                elif kind in ("q+", "k+"):
                    job, t = kind[0], p[2]
                    wait_apart(pool, read[job], count(b, 2, t + 1), passed["pool"])
                    nc.gpsimd.tensor_copy(parts[job][:, 1, t, :], rest[:, t, :]).then_inc(part_mid, 1)
                    wait(pool, part_mid, count(b, 4, t + (2 if job == "k" else 0) + 1))
                    nc.gpsimd.tensor_tensor(out=parts[job][:, 2, t, :], in0=rest[:, t, :],
                                            in1=parts[job][:, 1, t, :], op=ALU.subtract).then_inc(rest_split, 1)
                elif kind == "res":
                    wait(pool, res_loaded, count(b, 16, 16))
                    nc.gpsimd.tensor_tensor(out=res_t[:, :, :], in0=res_t[:, :, :],
                                            in1=bias[:, :].unsqueeze(1).broadcast_to([P, NT, D]),
                                            op=ALU.add).then_inc(res_done, 1)
                elif kind == "xs":
                    wait(pool, ln_done["ln2"], count(b, NT, NT))
                    wait_apart(pool, tok_stored, count(b, 16, 0), passed["pool"])
                    nc.gpsimd.tensor_copy(tok[:, :, 0:D], xn2[:, :, :]).then_inc(tok_hi, 1)
                    wait(pool, tok_hi, count(b, 1, 1))
                    nc.gpsimd.tensor_tensor(out=tok[:, :, D:2 * D], in0=xn2[:, :, :], in1=tok[:, :, 0:D],
                                            op=ALU.subtract).then_inc(tok_lo, 1)

            part_mid = sem("part_mid")
            nc.gpsimd.memset(ident[:, :], 0.0).then_inc(consts, 1)
            nc.gpsimd.memset(mask_qk[:, :], 0.0).then_inc(consts, 1)
            nc.gpsimd.memset(mask_kq[:, :], 0.0).then_inc(consts, 1)
            nc.gpsimd.memset(gwT[:, :, EXPERTS:32], 0.0).then_inc(consts, 1)
            nc.gpsimd.memset(minus_half[:, :], -0.5).then_inc(consts, 1)
            nc.gpsimd.memset(v_aug[:, :, :, :], 1.0).then_inc(consts, 1)
            pool.wait_ge(consts, 6)
            nc.gpsimd.affine_select(out=ident[:, :], in_=ident[:, :], compare_op=ALU.not_equal, fill=1.0,
                                    base=0, pattern=[[-1, P]], channel_multiplier=1).then_inc(consts, 1)
            nc.gpsimd.affine_select(out=mask_qk[:, :], in_=mask_qk[:, :], compare_op=ALU.is_ge, fill=NEG,
                                    base=0, pattern=[[-1, P]], channel_multiplier=1).then_inc(consts, 1)
            nc.gpsimd.affine_select(out=mask_kq[:, :], in_=mask_kq[:, :], compare_op=ALU.is_ge, fill=NEG,
                                    base=0, pattern=[[1, P]], channel_multiplier=-1).then_inc(consts, 1)
            pool.wait_ge(consts, CONSTS)
            piece(-1, ("ln1", 0, 1))
            pool.wait_ge(bias_done, 1)
            rounds(pool, piece)


def experts(nc, ctx, sb, sem, g):
    ident, identb, aff, tanh_g, passed = g["ident"], g["identb"], g["aff"], g["tanh_g"], g["passed"]
    bank, tok_dram = g["bank"], g["tok_dram"]
    out_rows = g["out"].rearrange("b t d -> (b t) d")
    gate_bank, up_bank, y_bank, tok_bank, w_bank = bank[0:2], bank[2:4], bank[4:6], bank[6], bank[7]

    CHUNK = BATCH // 4
    CHUNKS = BATCH // CHUNK
    IT = INNER // P
    WJOBS = 12
    ROUNDS = SLOTS // 8

    work = sb(ctx, "work", [P, T], F32)
    top = sb(ctx, "top", [P, SLOTS], F32)
    top_at = sb(ctx, "top_at", [P, SLOTS], U32)
    top_atf = sb(ctx, "top_atf", [P, SLOTS], F32)
    batch_base = sb(ctx, "batch_base", [P, EXPERTS * BATCH], F32)
    row_of = sb(ctx, "row_of", [P, EXPERTS * BATCH], U32)
    gating = sb(ctx, "gating", [P, EXPERTS * BATCH], F32)
    row_now = sb(ctx, "row_now", [P, 2, BATCH], U32)
    gate_now = sb(ctx, "gate_now", [P, 2, BATCH], F32)

    w_raw = {"gate": sb(ctx, "gate_raw", [P, IT, D], F32), "up": sb(ctx, "up_raw", [P, IT, D], F32),
             "down": sb(ctx, "down_raw", [P, NH2, INNER], F32)}
    w_in = {n: sb(ctx, f"{n}T", [P, 2, 2, NH2, INNER], BF16) for n in ("gate", "up")}
    w_out = sb(ctx, "downT", [P, 2, 2, IT, D], BF16)
    rows = sb(ctx, "rows", [P, 2, CHUNK, 2 * D], BF16)
    tokT = sb(ctx, "tokT", [P, 2, 2, NH2, T], BF16)
    silu = sb(ctx, "silu", [P, 2, T], F32)
    h32 = sb(ctx, "h32", [P, 2, T], F32)
    h = sb(ctx, "h", [P, 2, 2, IT, T], BF16)
    y = sb(ctx, "y", [P, 2, CHUNK, D], F32)

    names = ("rows_turned", "rows_copied", "top_found", "top_located", "top_taken", "at_float", "top_turned",
             "base_made", "row_made", "gating_made", "row_now_made", "gate_now_made", "w_turned", "w_copied", "w_hi", "w_lo",
             "tok_turned", "tok_read", "gate_filled", "up_filled", "silu_done", "h_done", "h_hi", "h_lo",
             "down_done", "y_read")
    S = {n: sem(n) for n in names}
    raw_loaded = {n: sem(f"{n}_raw_loaded") for n in w_raw}
    gathered = [[sem(f"gathered{i}{j}") for j in range(CHUNK)] for i in range(2)]
    scattered = [[sem(f"scattered{i}{j}") for j in range(CHUNK)] for i in range(2)]
    PARTS = ("gate", "up", "down")

    def schedule(pair):
        order = []
        for par in range(2):
            e = pair * 2 + par
            for c in range(CHUNKS):
                nxt = (e, par, c + 1) if c + 1 < CHUNKS else (e + 1, 1 - par, 0)
                aft = (e, par, c + 2) if c + 2 < CHUNKS else (e + 1, 1 - par, c + 2 - CHUNKS)
                last = (e, par, c - 1) if c else (e - 1, 1 - par, CHUNKS - 1)
                if c == 1:
                    order.append(("columns", e + 1, 1 - par, 0))
                order += [("gather", *aft, s) for s in range(CHUNK)]
                for it in range(IT):
                    order.append(("up", e, par, c, it))
                    if it in (0, 2, 4, 6):
                        order.append(("tok", *nxt, it // 2))
                    if it in (1, 3, 5):
                        order.append(("weights", e + 1, 1 - par, 0, 3 * c + it // 2))
                    if it == 7 and c in (1, 2, 3):
                        order.append(("load", e + 2, par, 0, PARTS[c - 1]))
                order += [("down", *last, s) for s in range(CHUNK)]
        return [p for p in order if not isinstance(p[1], int) or 0 <= p[1] < EXPERTS]

    def run(eng, piece, first, final):
        for p in first:
            piece(p)
        for p in schedule(0):
            piece(p)
        with eng.Fori(1, EXPERTS // 2 - 1) as pair:
            for p in schedule(pair):
                piece(p)
        for p in schedule(EXPERTS // 2 - 1):
            piece(p)
        for p in final:
            piece(p)

    BEFORE = ([("load", 0, 0, 0, n) for n in PARTS] + [("weights", 0, 0, 0, k) for k in range(WJOBS)]
              + [("load", 1, 1, 0, n) for n in PARTS] + [("columns", 0, 0, 0)]
              + [("gather", 0, 0, c, s) for c in range(2) for s in range(CHUNK)]
              + [("tok", 0, 0, 0, s) for s in range(CHUNK)])
    AFTER = [("down", EXPERTS - 1, 1, CHUNKS - 1, s) for s in range(CHUNK)]

    def is_first(e):
        return isinstance(e, int) and e == 0

    def weights_bank(e, k):
        return tok_bank if is_first(e) and k % 2 else w_bank

    def weights_dst(par, r, k):
        part, q = PARTS[k // 4], k % 4
        if part == "down":
            return w_out[:, par, r, 2 * q:2 * q + 2, :].rearrange("p i d -> p (i d)")
        return w_in[part][:, par, r, q // 2, (q % 2) * 512:(q % 2 + 1) * 512]

    with nc.Block() as block:
        @block.sync
        def _(sp):
            src = {"gate": g["w_gate"], "up": g["w_up"], "down": g["w_down"]}

            def piece(p):
                if p[0] == "load":
                    _, e, _, _, n = p
                    wait(sp, S["w_turned"], (e - 1) * WJOBS + 4 * (PARTS.index(n) + 1))
                    sp.dma_start(w_raw[n][:, :, :], src[n][e].rearrange("(o p) i -> p o i", p=P))\
                        .then_inc(raw_loaded[n], 16)

            run(sp, piece, BEFORE, AFTER)

        @block.gpsimd
        def _(pool):
            nc.gpsimd.iota(batch_base[:, :], pattern=[[0, EXPERTS], [T, BATCH]], base=0, channel_multiplier=0,
                           allow_small_or_imprecise_dtypes=True).then_inc(S["base_made"], 1)

            def piece(p):
                kind, e, par, c = p[:4]
                n = e * CHUNKS + c
                if kind == "weights" and is_first(e):
                    k = p[4]
                    wait(pool, S["w_copied"], k + 1)
                    wait(pool, S["w_hi"], k + 1)
                    nc.gpsimd.tensor_tensor(out=weights_dst(par, 1, k), in0=h32[:, k % 2, :],
                                            in1=weights_dst(par, 0, k), op=ALU.subtract).then_inc(S["w_lo"], 1)
                elif kind == "gather":
                    s = p[4]
                    if s == 0:
                        wait(pool, S["row_now_made"], e + 1)
                        wait_apart(pool, S["tok_turned"], (n - 1) * CHUNK, passed["pool"])
                    nc.gpsimd.indirect_dma_start(
                        rows[:, c % 2, s, :], None, tok_dram[:, :],
                        bass.IndirectOffsetOnAxis(ap=row_now[:, par, CHUNK * c + s:CHUNK * c + s + 1], axis=0))\
                        .then_inc(gathered[c % 2][s], 16)
                elif kind == "down":
                    s = p[4]
                    wait_apart(pool, S["y_read"], n * CHUNK + s + 1, passed["pool"])
                    nc.gpsimd.indirect_dma_start(
                        out_rows, bass.IndirectOffsetOnAxis(
                            ap=row_now[:, par, CHUNK * c + s:CHUNK * c + s + 1], axis=0),
                        y[:, c % 2, s, :], None, compute_op=ALU.add).then_inc(scattered[c % 2][s], 16)

            run(pool, piece, BEFORE, AFTER)
            for i in range(2):
                for s in range(CHUNK):
                    pool.wait_ge(scattered[i][s], 16 * EXPERTS * CHUNKS // 2)

        @block.tensor
        def _(pe):
            for i in range(NT):
                last = nc.tensor.transpose(gate_bank[0][:, i * P:(i + 1) * P], aff[:, i, :], ident[:, :])
            last.then_inc(S["rows_turned"], 1)

            def piece(p):
                kind, e, par, c = p[:4]
                n = e * CHUNKS + c
                if kind == "weights":
                    k = p[4]
                    part, q = PARTS[k // 4], k % 4
                    wait(pe, raw_loaded[part], (e + 1) * 16)
                    if is_first(e):
                        wait(pe, S["w_hi"], k - 1)
                    else:
                        wait(pe, S["w_lo"], e * WJOBS + k)
                    for j in range(4):
                        if part == "down":
                            it, dh = 2 * q + j // 2, j % 2
                            src = w_raw[part][:, dh, it * P:(it + 1) * P]
                        else:
                            dh, it = q // 2, 4 * (q % 2) + j
                            src = w_raw[part][:, it, dh * P:(dh + 1) * P]
                        last = nc.tensor.transpose(weights_bank(e, k)[:, j * P:(j + 1) * P], src, ident[:, :])
                    last.then_inc(S["w_turned"], 1)
                elif kind == "columns" and is_first(e):
                    pe.wait_ge(S["at_float"], 1)
                    pe.wait_ge(S["top_found"], ROUNDS)
                    nc.tensor.transpose(gate_bank[1][:, 0:P], top_atf[:, :], ident[:, :])
                    nc.tensor.transpose(gate_bank[1][:, P:2 * P], top[:, :], ident[:, :]).then_inc(S["top_turned"], 1)
                elif kind == "tok":
                    s = p[4]
                    wait(pe, gathered[c % 2][s], (e * 2 + c // 2 + 1) * 16)
                    wait(pe, S["tok_read"], n * CHUNK + s)
                    to = tok_bank[:, :].bitcast(BF16)
                    for j in range(4):
                        last = nc.tensor.transpose(to[:, j * P:(j + 1) * P], rows[:, c % 2, s, j * P:(j + 1) * P],
                                                   identb[:, :])
                    last.then_inc(S["tok_turned"], 1)
                elif kind == "up":
                    it = p[4]
                    m = n * IT + it
                    if it == 0:
                        wait(pe, S["tok_read"], (n + 1) * CHUNK)
                        wait(pe, S["w_lo"], (e + 1) * WJOBS)
                    for name, banks, freed, filled in (("gate", gate_bank, "silu_done", "gate_filled"),
                                                       ("up", up_bank, "h_done", "up_filled")):
                        wait(pe, S[freed], m - 1)
                        for dh in range(NH2):
                            hi, lo = (w_in[name][:, par, r, dh, it * P:(it + 1) * P] for r in range(2))
                            xh, xl = (tokT[:, c % 2, r, dh, :] for r in range(2))
                            nc.tensor.matmul(banks[it % 2][:, :], hi, xh, start=(dh == 0), stop=False)
                            nc.tensor.matmul(banks[it % 2][:, :], hi, xl, start=False, stop=False)
                            last = nc.tensor.matmul(banks[it % 2][:, :], lo, xh, start=False, stop=(dh == NH2 - 1))
                        last.then_inc(S[filled], 1)
                elif kind == "down":
                    s = p[4]
                    if s == 0:
                        wait(pe, S["h_lo"], (n + 1) * IT)
                    if s % 2 == 0:
                        wait(pe, S["y_read"], (n - 1) * CHUNK + s + 2)
                    to = y_bank[s // 2][:, (s % 2) * D:(s % 2 + 1) * D]
                    for it in range(IT):
                        hh, hl = (h[:, c % 2, r, it, s * P:(s + 1) * P] for r in range(2))
                        wh, wl = (w_out[:, par, r, it, :] for r in range(2))
                        nc.tensor.matmul(to, hh, wh, start=(it == 0), stop=False)
                        nc.tensor.matmul(to, hh, wl, start=False, stop=False)
                        last = nc.tensor.matmul(to, hl, wh, start=False, stop=(it == IT - 1))
                    last.then_inc(S["down_done"], 1)

            run(pe, piece, BEFORE, AFTER)

        @block.scalar
        def _(act):
            def piece(p):
                kind, e, par, c = p[:4]
                n = e * CHUNKS + c
                if kind == "weights":
                    k = p[4]
                    wait(act, S["w_turned"], e * WJOBS + k + 1)
                    if k == 0:
                        wait(act, S["up_filled"], (e - 1) * CHUNKS * IT)
                    if k == 8:
                        wait(act, S["down_done"], (e - 1) * CHUNKS * CHUNK)
                    if is_first(e):
                        wait(act, S["w_lo"], k - 1)
                        nc.scalar.activation(h32[:, k % 2, :], weights_bank(e, k)[:, :], ACT.Copy)\
                            .then_inc(S["w_copied"], 1)
                    nc.scalar.activation(weights_dst(par, 0, k), weights_bank(e, k)[:, :], ACT.Copy)\
                        .then_inc(S["w_hi"], 1)
                elif kind == "up":
                    it = p[4]
                    m = n * IT + it
                    wait(act, S["gate_filled"], m + 1)
                    wait(act, S["h_done"], m - 1)
                    nc.scalar.activation(silu[:, it % 2, :], gate_bank[it % 2][:, :], ACT.Silu)\
                        .then_inc(S["silu_done"], 1)
                    wait(act, S["h_done"], m + 1)
                    if it == 0:
                        wait(act, S["down_done"], (n - 1) * CHUNK)
                    nc.scalar.activation(h[:, c % 2, 0, it, :], h32[:, it % 2, :], ACT.Copy).then_inc(S["h_hi"], 1)
                elif kind == "down":
                    s = p[4]
                    if s % 2 == 0:
                        wait(act, S["down_done"], n * CHUNK + s + 2)
                    wait(act, scattered[c % 2][s], (e * 2 + c // 2) * 16)
                    col = CHUNK * c + s
                    nc.scalar.activation(y[:, c % 2, s, :], y_bank[s // 2][:, (s % 2) * D:(s % 2 + 1) * D],
                                         ACT.Copy, scale=gate_now[:, par, col:col + 1]).then_inc(S["y_read"], 1)

            run(act, piece, BEFORE, AFTER)

        @block.vector
        def _(dve):
            dve.wait_ge(S["rows_turned"], 1)
            nc.vector.tensor_copy(work[:, :], gate_bank[0][:, :]).then_inc(S["rows_copied"], 1)
            dve.wait_ge(S["rows_copied"], 1)
            for r in range(ROUNDS):
                at = slice(8 * r, 8 * r + 8)
                nc.vector.max(top[:, at], work[:, :]).then_inc(S["top_found"], 1)
                dve.wait_ge(S["top_found"], r + 1)
                nc.vector.max_index(top_at[:, at], top[:, at], work[:, :]).then_inc(S["top_located"], 1)
                dve.wait_ge(S["top_located"], r + 1)
                if r < ROUNDS - 1:
                    nc.vector.match_replace(work[:, :], top[:, at], work[:, :], -1.0).then_inc(S["top_taken"], 1)
                    dve.wait_ge(S["top_taken"], r + 1)
            nc.vector.tensor_copy(top_atf[:, :], top_at[:, :]).then_inc(S["at_float"], 1)

            def piece(p):
                kind, e, par, c = p[:4]
                n = e * CHUNKS + c
                if kind == "weights" and not is_first(e):
                    k = p[4]
                    wait(dve, S["w_hi"], e * WJOBS + k + 1)
                    nc.vector.tensor_tensor(weights_dst(par, 1, k), w_bank[:, :], weights_dst(par, 0, k),
                                            ALU.subtract).then_inc(S["w_lo"], 1)
                elif kind == "columns":
                    if is_first(e):
                        dve.wait_ge(S["top_turned"], 1)
                        dve.wait_ge(S["base_made"], 1)
                        nc.vector.tensor_tensor(row_of[:, :], gate_bank[1][:, 0:P], batch_base[:, :], ALU.add)\
                            .then_inc(S["row_made"], 1)
                        nc.vector.tensor_scalar(gating[:, :], gate_bank[1][:, P:2 * P], tanh_g[:, 1:2], None,
                                                ALU.mult).then_inc(S["gating_made"], 1)
                        dve.wait_ge(S["row_made"], 1)
                        dve.wait_ge(S["gating_made"], 1)
                    for s in range(CHUNK):
                        wait(dve, scattered[1][s], (e - 1) * 2 * 16)
                    cols = slice(e * BATCH, (e + 1) * BATCH) if isinstance(e, int) else bass.ds(e * BATCH, BATCH)
                    nc.vector.tensor_copy(row_now[:, par, :], row_of[:, cols]).then_inc(S["row_now_made"], 1)
                    nc.vector.tensor_copy(gate_now[:, par, :], gating[:, cols]).then_inc(S["gate_now_made"], 1)
                elif kind == "tok":
                    s = p[4]
                    wait(dve, S["tok_turned"], n * CHUNK + s + 1)
                    if s == 0:
                        wait(dve, S["up_filled"], (n - 1) * IT)
                    dst = tokT[:, c % 2, :, :, s * P:(s + 1) * P].rearrange("p r d t -> p (r d) t")
                    nc.vector.tensor_copy(dst, tok_bank[:, :].bitcast(BF16)[:, 0:4 * P].rearrange(
                        "p (j t) -> p j t", j=4)).then_inc(S["tok_read"], 1)
                elif kind == "up":
                    it = p[4]
                    m = n * IT + it
                    wait(dve, S["silu_done"], m + 1)
                    wait(dve, S["up_filled"], m + 1)
                    wait(dve, S["h_lo"], m - 1)
                    nc.vector.tensor_tensor(h32[:, it % 2, :], up_bank[it % 2][:, :], silu[:, it % 2, :], ALU.mult)\
                        .then_inc(S["h_done"], 1)
                    wait(dve, S["h_hi"], m + 1)
                    nc.vector.tensor_tensor(h[:, c % 2, 1, it, :], h32[:, it % 2, :], h[:, c % 2, 0, it, :],
                                            ALU.subtract).then_inc(S["h_lo"], 1)

            run(dve, piece, BEFORE, AFTER)


INPUTS = ["x", "ctx_1024", "g_xattn", "g_ffn", "L0_xattn_Wq", "L0_xattn_Wk", "L0_xattn_Wv", "L0_xattn_Wo",
          "L0_xattn_bo", "L0_ffn_gate_w", "L0_ffn_w_gate", "L0_ffn_w_up", "L0_ffn_w_down"]


def kernel(**inputs):
    import numpy as np
    import concourse.bacc as bacc
    from concourse.bass_utils import run_bass_kernel_spmd

    nc = bacc.Bacc("TRN2", target_bir_lowering=False, num_devices=1)
    arrays, args = {}, []
    for name in INPUTS:
        a = np.ascontiguousarray(inputs[name])
        arrays[f"in_{name}"] = a
        args.append(nc.dram_tensor(f"in_{name}", a.shape, mybir.dt.from_np(a.dtype), kind="ExternalInput").ap())
    args.append(nc.dram_tensor("out_0", (BATCH, T, D), F32, kind="ExternalOutput").ap())
    flamingo(nc, *args)
    r = run_bass_kernel_spmd(nc, [arrays], core_ids=[0])
    return r.results[0]["out_0"]
```
